# Optimizing a Trainium2 kernel written in Bass

```python
import numpy as np
import jax
import jax.numpy as jnp

def _softmax(x, axis=-1):
    return jax.nn.softmax(x, axis=axis)

def _gelu(x):
    return jax.nn.gelu(x, approximate=True)

def _silu(x):
    return jax.nn.silu(x)

def _sigmoid(x):
    return jax.nn.sigmoid(x)

def _layernorm(x, axis=-1, eps=1e-05):
    m = jnp.mean(x, axis=axis, keepdims=True)
    v = jnp.var(x, axis=axis, keepdims=True)
    return (x - m) / jnp.sqrt(v + eps)

def _scatter_add(tgt, idx, src, axis=0):
    return tgt.at[idx].add(src)

def _segment_sum(src, seg, n):
    return jax.ops.segment_sum(src, seg, n)
kernel_name = 'mk_adj_ffn_d1_adj_r2_529861'

def setup_inputs(seed: int=0):
    np.random.seed(seed)
    _w = jnp.asarray

    def _rec_inputs():
        import jax
        import jax.numpy as jnp
        _gk = jax.random.key(seed)
        x = -0.0005207 + 1.001 * jax.random.normal(jax.random.fold_in(_gk, 1), (4096, 128), jnp.float32)
        _a = jax.random.bernoulli(jax.random.fold_in(_gk, 2), 0.00390625, (4096, 4096))
        _a = jnp.logical_or(_a, jnp.eye(4096, dtype=bool))
        _af = _a.astype(jnp.float32)
        adj = _af
        return (x, adj)
    x, adj = _rec_inputs()

    def _L0_gnn_setup():
        import jax, jax.numpy as jnp
        import numpy as np
        N = 4096
        F = 128
        NEG_INF = -9000000000000000.0
        ALPHA = 0.2
        THRESH = 1e-06
        key = jax.random.key(seed)
        k1, k2, k3, k4 = jax.random.split(key, 4)
        x = jax.random.normal(k1, (N, F), jnp.float32)
        h0 = jax.random.normal(k2, (N, F), jnp.float32)
        limit = float(np.sqrt(6.0 / (2 * F + 1)) * 1.414)
        a = jax.random.uniform(k3, (2 * F, 1), jnp.float32, -limit, limit)
        temp = jnp.zeros((5,), jnp.float32)
        adj = jax.random.bernoulli(k4, 0.005, (N, N)).astype(jnp.float32)
        adj = jnp.maximum(adj, jnp.eye(N, dtype=jnp.float32))
        return {'x': x, 'h0': h0, 'a': a, 'temp': temp, 'adj': adj, 'l': 1}
    _L0_gnn_all = _L0_gnn_setup()
    _L0_gnn_in = {k: v for k, v in _L0_gnn_all.items() if k in ('h0', 'a', 'temp')}
    del _L0_gnn_all

    def _L0_ffn_setup():
        import jax, jax.numpy as jnp
        import numpy as np
        D_MODEL = 128
        D_STATE = 64
        D_CONV = 4
        EXPAND = 2
        HEADDIM = 64
        D_INNER = EXPAND * D_MODEL
        NHEADS = D_INNER // HEADDIM
        CONV_DIM = D_INNER + 2 * D_STATE
        D_IN_PROJ = 2 * D_INNER + 2 * D_STATE + NHEADS
        CHUNK = 128
        EPS = 1e-05

        def segsum(a):
            T = a.shape[-1]
            cs = jnp.cumsum(a, axis=-1)
            ss = cs[..., :, None] - cs[..., None, :]
            mask = jnp.tril(jnp.ones((T, T), dtype=bool))
            return jnp.where(mask, ss, -jnp.inf)

        def mamba2_block(x, W_in, conv_w, conv_b, dt_bias, A_log, D, norm_w, W_out, W_lin, b_lin):
            Bsz, L, _ = x.shape
            zxbcdt = x @ W_in
            z, xBC, dt = jnp.split(zxbcdt, [D_INNER, D_INNER + CONV_DIM], axis=-1)
            xp = jnp.pad(xBC, ((0, 0), (D_CONV - 1, 0), (0, 0)))
            conv = conv_b + sum((xp[:, k:k + L, :] * conv_w[:, k] for k in range(D_CONV)))
            xBC = jax.nn.silu(conv)
            xh, Bmat, Cmat = jnp.split(xBC, [D_INNER, D_INNER + D_STATE], axis=-1)
            dt = jax.nn.softplus(dt + dt_bias)
            A = -jnp.exp(A_log)
            nc = L // CHUNK
            xh = xh.reshape(Bsz, nc, CHUNK, NHEADS, HEADDIM)
            Bc = Bmat.reshape(Bsz, nc, CHUNK, D_STATE)
            Cc = Cmat.reshape(Bsz, nc, CHUNK, D_STATE)
            dtc = dt.reshape(Bsz, nc, CHUNK, NHEADS)
            dA = jnp.einsum('bclh,h->bhcl', dtc, A)
            A_cum = jnp.cumsum(dA, axis=-1)
            Lmat = jnp.exp(segsum(dA))
            xdt = xh * dtc[..., None]
            Y_diag = jnp.einsum('bcln,bcsn,bhcls,bcshp->bclhp', Cc, Bc, Lmat, xdt)
            decay_states = jnp.exp(A_cum[..., -1:] - A_cum)
            states = jnp.einsum('bcln,bhcl,bclhp->bchpn', Bc, decay_states, xdt)
            chunk_decay = jnp.exp(A_cum[..., -1])

            def step(h, inp):
                s, d = inp
                return (h * d[..., None, None] + s, h)
            _, prevs = jax.lax.scan(step, jnp.zeros_like(states[:, 0]), (jnp.moveaxis(states, 1, 0), jnp.moveaxis(chunk_decay, 2, 0)))
            prevs = jnp.moveaxis(prevs, 0, 1)
            Y_off = jnp.einsum('bcln,bchpn,bhcl->bclhp', Cc, prevs, jnp.exp(A_cum))
            Y = (Y_diag + Y_off + xh * D[:, None]).reshape(Bsz, L, D_INNER)
            Y = Y * jax.nn.silu(z)
            Y = Y * jax.lax.rsqrt(jnp.mean(Y * Y, axis=-1, keepdims=True) + EPS) * norm_w
            out = Y @ W_out
            return out @ W_lin + b_lin
        key = jax.random.key(seed)
        ks = jax.random.split(key, 12)
        B, L = (8, 2048)

        def gauss(k, shape, scale):
            return jax.random.normal(k, shape, dtype=jnp.float32) * scale
        return {'x': gauss(ks[0], (B, L, D_MODEL), 1.0), 'W_in': gauss(ks[1], (D_MODEL, D_IN_PROJ), D_MODEL ** (-0.5)), 'conv_w': gauss(ks[2], (CONV_DIM, D_CONV), 0.3), 'conv_b': gauss(ks[3], (CONV_DIM,), 0.1), 'dt_bias': jax.random.uniform(ks[4], (NHEADS,), minval=-4.0, maxval=-1.0), 'A_log': jnp.log(jax.random.uniform(ks[5], (NHEADS,), minval=1.0, maxval=16.0)), 'D': jnp.ones((NHEADS,), jnp.float32), 'norm_w': jnp.ones((D_INNER,), jnp.float32), 'W_out': gauss(ks[6], (D_INNER, D_MODEL), D_INNER ** (-0.5)), 'W_lin': gauss(ks[7], (D_MODEL, D_MODEL), D_MODEL ** (-0.5)), 'b_lin': jnp.zeros((D_MODEL,), jnp.float32)}
    _L0_ffn_all = _L0_ffn_setup()
    _L0_ffn_in = {k: v for k, v in _L0_ffn_all.items() if k in ('W_in', 'conv_w', 'conv_b', 'dt_bias', 'A_log', 'D', 'norm_w', 'W_out', 'W_lin', 'b_lin')}
    del _L0_ffn_all
    return {'x': x, 'adj': adj, 'L0_gnn_h0': _L0_gnn_in['h0'], 'L0_gnn_a': _L0_gnn_in['a'], 'L0_gnn_temp': _L0_gnn_in['temp'], 'L0_ffn_W_in': _L0_ffn_in['W_in'], 'L0_ffn_conv_w': _L0_ffn_in['conv_w'], 'L0_ffn_conv_b': _L0_ffn_in['conv_b'], 'L0_ffn_dt_bias': _L0_ffn_in['dt_bias'], 'L0_ffn_A_log': _L0_ffn_in['A_log'], 'L0_ffn_D': _L0_ffn_in['D'], 'L0_ffn_norm_w': _L0_ffn_in['norm_w'], 'L0_ffn_W_out': _L0_ffn_in['W_out'], 'L0_ffn_W_lin': _L0_ffn_in['W_lin'], 'L0_ffn_b_lin': _L0_ffn_in['b_lin']}

def reference(x, adj, L0_gnn_h0, L0_gnn_a, L0_gnn_temp, L0_ffn_W_in, L0_ffn_conv_w, L0_ffn_conv_b, L0_ffn_dt_bias, L0_ffn_A_log, L0_ffn_D, L0_ffn_norm_w, L0_ffn_W_out, L0_ffn_W_lin, L0_ffn_b_lin):
    import jax
    import jax.numpy as jnp

    def _L0_gnn_ref(x, h0, a, temp, adj, l):
        import jax, jax.numpy as jnp
        import numpy as np
        N = 4096
        F = 128
        NEG_INF = -9000000000000000.0
        ALPHA = 0.2
        THRESH = 1e-06
        Fdim = x.shape[1]
        feat_1 = x @ a[:Fdim]
        feat_2 = x @ a[Fdim:]
        e = jax.nn.leaky_relu(feat_1 + feat_2.T, ALPHA)
        att = jnp.where(adj > 0, e, NEG_INF)
        U = jax.nn.softmax(att, axis=1)
        P = 0.5 * U
        prop_u = U @ x
        rowsum = jnp.sum(U * P, axis=1)
        coe = jax.nn.sigmoid(temp)
        xi = x * rowsum[:, None]
        feat_odd = prop_u - xi
        feat_even = x + prop_u - xi
        feat = coe[2] * feat_odd + (1.0 - coe[2]) * feat_even
        sgn = jnp.sign(feat)
        mod = jnp.abs(feat)
        mod = jnp.where(mod > THRESH, mod - THRESH, 0.0)
        feat = mod * sgn
        pu = U @ feat
        feat_odd2 = feat - coe[3] * pu
        feat_even2 = pu + feat_odd2 * rowsum[:, None]
        feat_odd2 = coe[0] * feat_odd2 + (1.0 - coe[0]) * h0
        out = coe[1] * feat_even2 + (1.0 - coe[1]) * feat_odd2
        return out

    def _L0_ffn_ref(x, W_in, conv_w, conv_b, dt_bias, A_log, D, norm_w, W_out, W_lin, b_lin):
        import jax, jax.numpy as jnp
        import numpy as np
        D_MODEL = 128
        D_STATE = 64
        D_CONV = 4
        EXPAND = 2
        HEADDIM = 64
        D_INNER = EXPAND * D_MODEL
        NHEADS = D_INNER // HEADDIM
        CONV_DIM = D_INNER + 2 * D_STATE
        D_IN_PROJ = 2 * D_INNER + 2 * D_STATE + NHEADS
        CHUNK = 128
        EPS = 1e-05

        def segsum(a):
            T = a.shape[-1]
            cs = jnp.cumsum(a, axis=-1)
            ss = cs[..., :, None] - cs[..., None, :]
            mask = jnp.tril(jnp.ones((T, T), dtype=bool))
            return jnp.where(mask, ss, -jnp.inf)

        def mamba2_block(x, W_in, conv_w, conv_b, dt_bias, A_log, D, norm_w, W_out, W_lin, b_lin):
            Bsz, L, _ = x.shape
            zxbcdt = x @ W_in
            z, xBC, dt = jnp.split(zxbcdt, [D_INNER, D_INNER + CONV_DIM], axis=-1)
            xp = jnp.pad(xBC, ((0, 0), (D_CONV - 1, 0), (0, 0)))
            conv = conv_b + sum((xp[:, k:k + L, :] * conv_w[:, k] for k in range(D_CONV)))
            xBC = jax.nn.silu(conv)
            xh, Bmat, Cmat = jnp.split(xBC, [D_INNER, D_INNER + D_STATE], axis=-1)
            dt = jax.nn.softplus(dt + dt_bias)
            A = -jnp.exp(A_log)
            nc = L // CHUNK
            xh = xh.reshape(Bsz, nc, CHUNK, NHEADS, HEADDIM)
            Bc = Bmat.reshape(Bsz, nc, CHUNK, D_STATE)
            Cc = Cmat.reshape(Bsz, nc, CHUNK, D_STATE)
            dtc = dt.reshape(Bsz, nc, CHUNK, NHEADS)
            dA = jnp.einsum('bclh,h->bhcl', dtc, A)
            A_cum = jnp.cumsum(dA, axis=-1)
            Lmat = jnp.exp(segsum(dA))
            xdt = xh * dtc[..., None]
            Y_diag = jnp.einsum('bcln,bcsn,bhcls,bcshp->bclhp', Cc, Bc, Lmat, xdt)
            decay_states = jnp.exp(A_cum[..., -1:] - A_cum)
            states = jnp.einsum('bcln,bhcl,bclhp->bchpn', Bc, decay_states, xdt)
            chunk_decay = jnp.exp(A_cum[..., -1])

            def step(h, inp):
                s, d = inp
                return (h * d[..., None, None] + s, h)
            _, prevs = jax.lax.scan(step, jnp.zeros_like(states[:, 0]), (jnp.moveaxis(states, 1, 0), jnp.moveaxis(chunk_decay, 2, 0)))
            prevs = jnp.moveaxis(prevs, 0, 1)
            Y_off = jnp.einsum('bcln,bchpn,bhcl->bclhp', Cc, prevs, jnp.exp(A_cum))
            Y = (Y_diag + Y_off + xh * D[:, None]).reshape(Bsz, L, D_INNER)
            Y = Y * jax.nn.silu(z)
            Y = Y * jax.lax.rsqrt(jnp.mean(Y * Y, axis=-1, keepdims=True) + EPS) * norm_w
            out = Y @ W_out
            return out @ W_lin + b_lin
        return mamba2_block(x, W_in, conv_w, conv_b, dt_bias, A_log, D, norm_w, W_out, W_lin, b_lin)
    x = x + _L0_gnn_ref(_layernorm(x, axis=-1), L0_gnn_h0, L0_gnn_a, L0_gnn_temp, adj, 1)
    x = x + _L0_ffn_ref(_layernorm(x, axis=-1)[None], L0_ffn_W_in, L0_ffn_conv_w, L0_ffn_conv_b, L0_ffn_dt_bias, L0_ffn_A_log, L0_ffn_D, L0_ffn_norm_w, L0_ffn_W_out, L0_ffn_W_lin, L0_ffn_b_lin)[0]
    return x

_drawn_inputs = setup_inputs


def setup_inputs(seed=0):
    import zlib

    import numpy as np

    out = dict(_drawn_inputs(seed))
    spreads = {'L0_gnn_temp': (0.0, 0.8),
     'L0_ffn_D': (1.0, 0.2),
     'L0_ffn_norm_w': (1.0, 0.2),
     'L0_ffn_b_lin': (0.0, 0.1)}
    factors = {'L0_ffn_A_log': 7.209}
    for name, (base, spread) in spreads.items():
        noise = np.random.default_rng([zlib.crc32(name.encode()), seed]).standard_normal(out[name].shape)
        drawn = base * np.exp(spread * noise) if base else spread * noise
        out[name] = jnp.asarray(drawn.astype(out[name].dtype))
    for name, factor in factors.items():
        out[name] = (out[name] * factor).astype(out[name].dtype)
    return out
```

```python
from contextlib import ExitStack

import numpy as np

import concourse.bass as bass
from concourse import mybir

F32 = mybir.dt.float32
F32R = mybir.dt.float32r
BF16 = mybir.dt.bfloat16
I8 = mybir.dt.int8
ALU = mybir.AluOpType
ACT = mybir.ActivationFunctionType
AX_X = mybir.AxisListType.X

P = 128
SHIFT = 30.0
THRESH = 1e-06
EPS = 1e-05
SLOPE = 0.2


def gnn_ffn_kernel(nc, x, adj, h0, a, temp, W_in, conv_w, conv_b, dt_bias, A_log, D, norm_w, W_out, W_lin, b_lin, out):
    N, F = x.shape
    NT = N // P
    IT = 4
    NG = NT // IT
    JB = 8
    NB = NT // JB
    BLOCKS = IT * NB
    JH = NT // BLOCKS
    XC = F + 2
    MASKS = 4
    TRB = 4
    assert F == P and NG % 2 == 0

    x_v = x.rearrange("(t p) f -> p t f", p=P)
    h0_v = h0.rearrange("(t p) f -> t p f", p=P)
    out_v = out.rearrange("(t p) f -> t p f", p=P)
    xt_v = x.rearrange("(t p) f -> t p f", p=P)
    adj_v = adj.rearrange("(g i p) j -> g p i j", i=IT, p=P)
    code_dram = nc.dram_tensor("edge_codes", (NT, P, NT * P), I8, kind="Internal").ap()

    with ExitStack() as ctx:
        def sb(name, shape, dt=F32):
            return ctx.enter_context(nc.sbuf_tensor(name, shape, dt))

        def sem(name):
            return ctx.enter_context(nc.semaphore(name))

        def psum(name, shape, dt=F32):
            return ctx.enter_context(nc.psum_tensor(name, shape, dt))

        adj_in = sb("adj_in", [P, 2, IT, 4 * P])
        edges = sb("edges", [P, 4, IT, 2 * P], BF16)
        code = sb("code", [P, 2, IT, NT * P], I8)
        maskA = sb("maskA", [P, MASKS, JB * P], F32R)
        maskC = sb("maskC", [P, MASKS, JB * P], F32R)
        Y = sb("Y", [P, NT, 2, 2, XC], F32R)
        f1_rows = sb("f1_rows", [P, N])
        xn = sb("xn", [P, NT, F])
        xnT = code[:, 1, :, :].rearrange("p i j -> p (i j)").bitcast(F32)
        ywork = sb("ywork", [P, 2 * JB * XC])

        ident = sb("ident", [P, P])
        ident2 = sb("ident2", [P, P], BF16)
        ones = sb("ones", [P, P])
        a_col = sb("a_col", [P, 2])
        a1_wide = sb("a1_wide", [P, P])
        col_mean = sb("col_mean", [P, F])
        stats = sb("stats", [P, NT, 6])
        mv = sb("mv", [P, NT, 2])
        rstd = sb("rstd", [P, NT])
        consts = sb("consts", [P, 4, NT])
        fcol = sb("fcol", [P, NT, 2])
        neg_f2 = sb("neg_f2", [P, NT])
        grow = sb("grow", [P, 8])
        colw = sb("colw", [P, 2, NT, 2])
        roww = sb("roww", [P, NT, 2])
        hcol = sb("hcol", [P, 2, NT])
        coef = sb("coef", [P, 12])
        acc_s = sb("acc_s", [P, 2, 2, XC])
        ps_sum = sb("ps_sum", [P, 2, 2, XC])
        q_c = sb("q_c", [P, 2, 2])
        k_one = sb("k_one", [P, 2, 1])
        num = sb("num", [P, XC])
        small = sb("small", [P, 24])
        row_out = sb("row_out", [P, NT, 4])
        featw = sb("featw", [P, 3, F])
        scaled = sb("scaled", [P, 2, F])
        fwork = sb("fwork", [P, 2, F])
        class Space:
            def __init__(self, flat):
                self.flat, self.at = flat, 0

            def take(self, *shape):
                n = 1
                for d in shape:
                    n *= d
                assert self.at + n <= self.flat.shape[1], shape
                v = self.flat[:, self.at:self.at + n]
                self.at += n
                if len(shape) == 1:
                    return v
                names = "abcd"[:len(shape)]
                sizes = {names[i]: shape[i] for i in range(len(shape) - 1)}
                return v.rearrange(f"p ({' '.join(names)}) -> p {' '.join(names)}", **sizes)

        rows_space = Space(f1_rows[:, :])
        adj_space = Space(adj_in[:, :, :, :].rearrange("p a b c -> p (a b c)"))
        code_space = Space(code[:, 1, :, :].rearrange("p i j -> p (i j)").bitcast(F32))

        y_space = Space(ywork[:, :])

        DI = W_out.shape[0]
        NH = dt_bias.shape[0]
        HD = DI // NH
        DS = (conv_w.shape[0] - DI) // 2
        TAPS = conv_w.shape[1]
        CB = conv_w.shape[0] // P
        KB = DI // P
        w_zdt = rows_space.take(DI + NH)
        w_xbc = rows_space.take(CB * P)
        w_out = rows_space.take(KB, P)
        w_outT = rows_space.take(KB, P)
        w_lin = rows_space.take(P)
        w_comb = rows_space.take(KB, P)
        conv_wt = rows_space.take(CB, TAPS)
        conv_bt = rows_space.take(CB)
        normw = rows_space.take(KB)
        b_row = rows_space.take(P)
        dt_b = rows_space.take(NH)
        a_row = rows_space.take(NH)
        d_row = rows_space.take(NH)
        upto = rows_space.take(P)
        after = rows_space.take(P)
        x_in = adj_space.take(2, F)
        h0_in = adj_space.take(2, F)
        base = adj_space.take(2, F)
        x1 = adj_space.take(2, F)
        x1b = adj_space.take(4, F)
        xn2 = adj_space.take(2, F)
        xn2T = adj_space.take(F)
        outb = adj_space.take(2, F)
        hist = adj_space.take(2, CB, P + TAPS - 1)
        conv = code_space.take(CB, P)
        gate_t = code_space.take(CB, P)
        xbc = code_space.take(2, CB, P)
        xl = code_space.take(CB * P)
        zdt = code_space.take(DI + NH)
        ztan = y_space.take(DI)
        cT = adj_space.take(P)
        gate = rows_space.take(2, DI)
        dam = rows_space.take(NH, P)
        expD = code_space.take(NH, P)
        gm = adj_space.take(P)
        wmix = code_space.take(NH, P)
        xdt = adj_space.take(DI)
        xdtd = rows_space.take(DI)
        xD = adj_space.take(DI)
        yg = rows_space.take(DI)
        yT = adj_space.take(KB, P)
        state = code_space.take(2, DI)
        pstate = y_space.take(DI)
        ysum = y_space.take(DI)
        junk = y_space.take(DI)
        sum2 = y_space.take(2 * F)
        tiny = rows_space.take(16, 8)

        ps = [psum(f"ps{i}", [P, 512]) for i in range(4)]
        accA = [psum(f"accA{i}", [P, 512]) for i in range(2)]
        accC = [psum(f"accC{i}", [P, 512]) for i in range(2)]

        names = """x_in0 x_in1 x_in2 x_in3 small_in const_ready stats_done rstd_done norm_done xT_done xT_copied
            fcol_done f2_copied fmax_done shift_done roww_done colw_done f1_done f1_copied ysum_done colmean_done coef_done
            a1_ready y_prod y_hi y_done adj_in0 adj_in1 signed tr_done coded maskA_ready maskC_ready mm_done acc_read summed
            spilled scaled_done feat_done pch vch codes_in0 codes_in1 codes_in2 codes_in3 y2_prod y2_hi y2_done
            rowx_in0 rowx_in1 base_done x1_done x1b_done stored0 stored1 w_in w_ready w_turned w_copied w_mult w_done
            ln_done rstd2 xn2_ready p_xT p_in p_cum p_tr p_ct p_g p_y p_yT p_o xT_ready xl_ready in_read
            zt_ready nv_ready ew_ready dt_ready dam_ready conv_pre ctan_ready conv_ready halo_done gate_done
            cT_ready mix_ready xdt_ready xD_ready ps_ready y_read yg_ready st_done yT_ready ssq_ready rs_ready
            exp_done out_done zcopy""".split()
        S = {n: sem(n) for n in names}
        block = ctx.enter_context(nc.Block())
        R1 = NG * BLOCKS
        LEAD = 2
        SLOTS = 4

        def wait(eng, name, value):
            if not isinstance(value, int) or value > 0:
                eng.wait_ge(S[name], value)

        def code_count(n, k, b):
            return (n - b - k * NB) + 16 if not isinstance(n, int) else (n - b - k * NB) // NB // SLOTS * 16 + 16

        def schedule(eng, slot):
            def fixed(s_):
                slot(s_, s_ % SLOTS, s_ < NT, s_ + 1 < NT, [0 <= s_ - d < NT for d in (1, 2, 3, 4)])

            for s_ in range(SLOTS):
                fixed(s_)
            with eng.Fori(0, NT // SLOTS - 2) as u:
                for k in range(SLOTS):
                    slot(u * SLOTS + (k + SLOTS), k, True, True, [True] * 4)
            for s_ in range(NT - SLOTS, NT + 4):
                fixed(s_)


        XCH = 4
        TPC = NT // XCH
        NUM4 = 4 * P

        @block.sync
        def _(sp):
            for k in range(XCH):
                sp.dma_start(xn[:, k * TPC:(k + 1) * TPC, :], x_v[:, k * TPC:(k + 1) * TPC, :]).then_inc(S[f"x_in{k}"], 16)
            sp.dma_start(a_col[:], a.rearrange("(c p) o -> p (c o)", p=P), allow_slow_non_contiguous=True).then_inc(S["small_in"], 16)
            sp.dma_start(grow[:, 0:5], temp.rearrange("(o c) -> o c", o=1).broadcast_to([P, 5])).then_inc(S["small_in"], 16)

            def load_adj(G, c, wait=True):
                row = sp.snap(G) if not isinstance(G, int) else G
                if wait:
                    sp.wait_ge(S["signed"], (G * 8 + (c - 1)) * 2)
                src = adj_v[bass.ds(row, 1), :, :, c * NUM4:(c + 1) * NUM4].rearrange("g p i j -> (g p) i j")
                sp.dma_start(adj_in[:, c % 2], src).then_inc(S[f"adj_in{c % 2}"], 16)

            def spill(G, par):
                row = sp.snap(G * IT) if not isinstance(G, int) else G * IT
                sp.wait_ge(S["coded"], (G + 1) * NT)
                dst = code_dram[bass.ds(row, IT)].rearrange("i p j -> p i j")
                sp.dma_start(dst, code[:, par]).then_inc(S["spilled"], 16)

            for c in range(8):
                load_adj(0, c, wait=c >= 2)
            for c in range(4):
                load_adj(1, c)
            spill(0, 0)
            for c in range(4, 8):
                load_adj(1, c)
            with nc.sync.Fori(1, NG // 2) as u:
                for par in range(2):
                    for c in range(4):
                        load_adj(u * 2 + par, c)
                    spill(u * 2 + (par - 1), 1 - par)
                    for c in range(4, 8):
                        load_adj(u * 2 + par, c)
            spill(NG - 1, 1)

            sp.wait_ge(S["coded"], NG * NT)
            zw = DI + CB * P
            sp.dma_start(w_zdt[:, 0:DI], W_in[:, 0:DI]).then_inc(S["w_in"], 16)
            sp.dma_start(w_zdt[:, DI:DI + NH], W_in[:, zw:zw + NH]).then_inc(S["w_in"], 16)
            sp.dma_start(w_xbc, W_in[:, DI:zw]).then_inc(S["w_in"], 16)
            sp.dma_start(w_out, W_out.rearrange("(k p) n -> p k n", p=P)).then_inc(S["w_in"], 16)
            sp.dma_start(w_lin, W_lin).then_inc(S["w_in"], 16)
            sp.dma_start(conv_wt, conv_w.rearrange("(k p) n -> p k n", p=P)).then_inc(S["w_in"], 16)
            sp.dma_start(conv_bt, conv_b.rearrange("(k p) -> p k", p=P), allow_slow_non_contiguous=True).then_inc(S["w_in"], 16)
            sp.dma_start(normw, norm_w.rearrange("(k p) -> p k", p=P), allow_slow_non_contiguous=True).then_inc(S["w_in"], 16)
            for dst, src, n in ((b_row, b_lin, P), (dt_b, dt_bias, NH), (a_row, A_log, NH), (d_row, D, NH)):
                sp.dma_start(dst, src.rearrange("(o c) -> o c", o=1).broadcast_to([P, n])).then_inc(S["w_in"], 16)

            def load_codes(T, k):
                row = sp.snap(T) if not isinstance(T, int) else T
                if not isinstance(T, int) or T >= SLOTS:
                    taken = sp.snap((T - SLOTS + 1) * NB + R1) if not isinstance(T, int) else (T - SLOTS + 1) * NB + R1
                    sp.wait_ge(S["maskA_ready"], taken)
                    sp.wait_ge(S["maskC_ready"], taken)
                sp.dma_start(code[:, 0, k, :], code_dram[bass.ds(row, 1)].rearrange("i p j -> (i p) j")).then_inc(S[f"codes_in{k}"], 16)

            def load_rows(T, k):
                row = sp.snap(T) if not isinstance(T, int) else T
                wait(sp, "base_done", T - 1)
                sp.dma_start(x_in[:, k], xt_v[bass.ds(row, 1)].rearrange("i p j -> (i p) j")).then_inc(S[f"rowx_in{k}"], 16)
                sp.dma_start(h0_in[:, k], h0_v[bass.ds(row, 1)].rearrange("i p j -> (i p) j")).then_inc(S[f"rowx_in{k}"], 16)

            def store(T, k):
                row = sp.snap(T) if not isinstance(T, int) else T
                sp.wait_ge(S["out_done"], T + 1)
                sp.dma_start(out_v[bass.ds(row, 1)].rearrange("i p j -> (i p) j"), outb[:, k]).then_inc(S[f"stored{k}"], 16)

            sp.wait_ge(S["spilled"], 16 * NG)
            sp.wait_ge(S["maskA_ready"], R1 - BLOCKS)
            sp.wait_ge(S["maskC_ready"], R1 - BLOCKS)
            for T in range(SLOTS - 1):
                load_codes(T, T)
            load_rows(0, 0)

            def slot(s_, k, now, then, ok):
                if not isinstance(s_, int) or s_ + SLOTS - 1 < NT:
                    load_codes(s_ + (SLOTS - 1), (k + SLOTS - 1) % SLOTS)
                if then:
                    load_rows(s_ + 1, (k + 1) % 2)
                if ok[3]:
                    store(s_ - 4, k % 2)

            schedule(nc.sync, slot)
            sp.wait_ge(S["stored0"], 8 * NT)
            sp.wait_ge(S["stored1"], 8 * NT)

        @block.gpsimd
        def _(pool):
            g = nc.gpsimd
            chain = [0]

            def link(ins):
                chain[0] += 1
                ins.then_inc(S["pch"], 1)
                pool.wait_ge(S["pch"], chain[0])

            def end_chain():
                g.sem_clear(S["pch"])
                chain[0] = 0

            g.memset(consts[:, 0], -0.5)
            g.memset(consts[:, 1], -1.0)
            g.memset(consts[:, 2], EPS)
            g.memset(consts[:, 3], EPS * DI)
            g.memset(ones[:], 1.0)
            g.memset(ident2[:], 0.0)
            link(g.memset(ident[:], 0.0))
            g.affine_select(out=ident2[:], in_=ident2[:], compare_op=ALU.not_equal, fill=2.0, base=0,
                            pattern=[[-1, P]], channel_multiplier=1)
            g.affine_select(out=ident[:], in_=ident[:], compare_op=ALU.not_equal, fill=1.0, base=0,
                            pattern=[[-1, P]], channel_multiplier=1).then_inc(S["const_ready"], 1)
            pool.wait_ge(S["stats_done"], 1)
            link(g.tensor_scalar(rstd[:], mv[:, :, 1], EPS, None, ALU.add))
            g.tensor_tensor(rstd[:], rstd[:], consts[:, 0], ALU.pow).then_inc(S["rstd_done"], 1)
            pool.wait_ge(S["coef_done"], 1)
            link(g.tensor_scalar(coef[:, 0:5], grow[:, 0:5], 1.0, None, ALU.add))
            link(g.tensor_tensor(coef[:, 0:5], coef[:, 0:5], consts[:, 1, 0:5], ALU.pow))
            link(g.tensor_scalar(coef[:, 5:6], coef[:, 2:3], -1.0, 1.0, ALU.mult, ALU.add))
            link(g.tensor_scalar(coef[:, 6:7], coef[:, 1:2], -1.0, 1.0, ALU.mult, ALU.add))
            link(g.tensor_scalar(coef[:, 7:8], coef[:, 0:1], -1.0, 1.0, ALU.mult, ALU.add))
            link(g.tensor_tensor(coef[:, 8:9], coef[:, 6:7], coef[:, 0:1], ALU.mult))
            link(g.tensor_tensor(coef[:, 9:10], coef[:, 6:7], coef[:, 7:8], ALU.mult))
            g.tensor_scalar(coef[:, 10:11], coef[:, 3:4], -1.0, None, ALU.mult).then_inc(S["coef_done"], 1)
            pool.wait_ge(S["fmax_done"], 1)
            g.partition_all_reduce(grow[:, 6:7], grow[:, 5:6], P, bass.bass_isa.ReduceOp.max).then_inc(S["shift_done"], 1)
            end_chain()

            def features(T, k):
                row = g.snap(T) if not isinstance(T, int) else T
                n = {q: small[:, i:i + 1] for i, q in enumerate("E e r zn rho q qz rr s".split())}
                wait(pool, "summed", T + 1)
                pool.wait_ge(S["roww_done"], 1)
                link(g.tensor_copy(small[:, 0:2], roww[:, bass.ds(row, 1), :].rearrange("p a b -> p (a b)")))
                link(g.tensor_tensor(small[:, 12:14], acc_s[:, k, :, F + 1], small[:, 0:1].broadcast_to([P, 2]), ALU.mult))
                link(g.tensor_tensor(num[:], ps_sum[:, k, 0], ps_sum[:, k, 1], ALU.add))
                link(g.tensor_tensor(small[:, 14:16], small[:, 12:14], q_c[:, k], ALU.add))
                link(g.tensor_tensor(n["q"], small[:, 14:15], small[:, 15:16], ALU.add))
                link(g.tensor_scalar(n["zn"], num[:, F:F + 1], 0.0, float(N), ALU.is_equal, ALU.mult))
                link(g.tensor_tensor(n["s"], num[:, F:F + 1], n["zn"], ALU.add))
                link(g.tensor_tensor(n["r"], n["s"], consts[:, 1, 0:1], ALU.pow))
                link(g.tensor_tensor(n["qz"], n["q"], n["zn"], ALU.add))
                link(g.tensor_tensor(n["rr"], n["r"], n["r"], ALU.mult))
                link(g.tensor_tensor(n["rho"], n["qz"], n["rr"], ALU.mult))
                link(g.tensor_scalar(n["rho"], n["rho"], 0.5, None, ALU.mult))
                wait(pool, "feat_done", T - 1)
                link(g.tensor_tensor(k_one[:, k], coef[:, 5:6], n["rho"], ALU.subtract))
                link(g.tensor_tensor(featw[:, 0], col_mean[:], n["zn"].broadcast_to([P, F]), ALU.mult))
                link(g.tensor_tensor(featw[:, 1], featw[:, 0], num[:, 0:F], ALU.add))
                link(g.tensor_tensor(scaled[:, k], featw[:, 1], n["r"].broadcast_to([P, F]), ALU.mult))
                link(g.tensor_copy(row_out[:, bass.ds(row, 1), :].rearrange("p a b -> p (a b)"), small[:, 2:6]))
                end_chain()
                g.sem_inc(S["scaled_done"], 1)

            pool.wait_ge(S["colmean_done"], 1)
            features(0, 0)
            features(1, 1)
            with g.Fori(1, NT // 2) as u:
                for k in range(2):
                    features(u * 2 + k, k)

            pool.wait_ge(S["coded"], NG * NT)
            pool.wait_ge(S["signed"], NG * BLOCKS)
            g.affine_select(out=upto, in_=ones[:], compare_op=ALU.is_ge, fill=0.0, base=0, pattern=[[1, P]], channel_multiplier=-1)
            g.affine_select(out=after, in_=ones[:], compare_op=ALU.is_gt, fill=0.0, base=0, pattern=[[-1, P]], channel_multiplier=1)
            pool.wait_ge(S["spilled"], NG * 16)
            pool.wait_ge(S["maskA_ready"], R1)
            pool.wait_ge(S["maskC_ready"], R1)
            g.memset(state[0:DS, 0], 0.0)
            g.memset(hist[:, 0, :, 0:TAPS - 1], 0.0).then_inc(S["halo_done"], 1)

            def base_of(s_, k):
                row = g.snap(s_) if not isinstance(s_, int) else s_
                kap, w, wz = small[:, 12:13], small[:, 14 + k % 2:15 + k % 2], small[:, 13:14]
                wait(pool, f"rowx_in{k % 2}", (s_ - k % 2) * 16 + 32)
                pool.wait_ge(S["colmean_done"], 2)
                pool.wait_ge(S["feat_done"], NT)
                link(g.tensor_copy(small[:, 8:12], row_out[:, bass.ds(row, 1), :].rearrange("p a b -> p (a b)")))
                r, zn, rho = (small[:, i:i + 1] for i in (8, 9, 10))
                link(g.tensor_tensor(kap, coef[:, 1:2], rho, ALU.mult))
                link(g.tensor_tensor(kap, kap, coef[:, 8:9], ALU.add))
                link(g.tensor_tensor(wz, kap, coef[:, 10:11], ALU.mult))
                link(g.tensor_tensor(wz, wz, coef[:, 1:2], ALU.add))
                wait(pool, "x1_done", s_ - 1)
                link(g.tensor_tensor(w, wz, r, ALU.mult))
                link(g.tensor_tensor(wz, w, zn, ALU.mult))
                link(g.tensor_tensor(featw[:, 0], xn[:, bass.ds(row, 1), :].rearrange("p a b -> p (a b)"),
                                     kap.broadcast_to([P, F]), ALU.mult))
                link(g.tensor_tensor(featw[:, 1], h0_in[:, k % 2], coef[:, 9:10].broadcast_to([P, F]), ALU.mult))
                link(g.tensor_tensor(featw[:, 0], featw[:, 0], featw[:, 1], ALU.add))
                link(g.tensor_tensor(featw[:, 0], featw[:, 0], x_in[:, k % 2], ALU.add))
                link(g.tensor_tensor(featw[:, 1], col_mean[:], wz.broadcast_to([P, F]), ALU.mult))
                link(g.tensor_tensor(base[:, k % 2], featw[:, 0], featw[:, 1], ALU.add))
                g.sem_inc(S["base_done"], 1)

            def heads(ap, width):
                return ap.rearrange("p (h w) -> p h w", h=NH)

            def slot(s_, k, now, then, ok):
                if now:
                    base_of(s_, k)
                if ok[0]:
                    kt = (k - 1) % SLOTS
                    wait(pool, "ln_done", s_)
                    wait(pool, "xn2_ready", s_ - 1)
                    link(g.tensor_tensor(tiny[:, 1, 0:1], tiny[:, 0, 1:2], consts[:, 2, 0:1], ALU.add))
                    g.tensor_tensor(tiny[:, 1, 1:2], tiny[:, 1, 0:1], consts[:, 0, 0:1], ALU.pow).then_inc(S["rstd2"], 1)
                    wait(pool, "out_done", s_ - 4)
                    g.tensor_tensor(x1b[:, kt], x1[:, kt % 2], b_row, ALU.add).then_inc(S["x1b_done"], 1)
                if ok[2]:
                    kc = (k - 3) % SLOTS
                    wait(pool, "xl_ready", s_ - 2)
                    wait(pool, "p_y", s_ - 3)
                    dtc = tiny[:, 2 + kc % 2, 0:NH]
                    link(g.tensor_tensor(heads(xdt, HD), heads(xl[:, 0:DI], HD), dtc.unsqueeze(2).broadcast_to([P, NH, HD]), ALU.mult))
                    wait(pool, "exp_done", s_ - 2)
                    g.tensor_tensor(heads(xdtd, HD), heads(xdt, HD), expD[:, :, P - 1:P].broadcast_to([P, NH, HD]), ALU.mult).then_inc(S["xdt_ready"], 1)
                    wait(pool, "y_read", s_ - 3)
                    g.tensor_tensor(heads(xD, HD), heads(xl[:, 0:DI], HD), d_row.unsqueeze(2).broadcast_to([P, NH, HD]), ALU.mult).then_inc(S["xD_ready"], 1)
                    wait(pool, "st_done", s_ - 3)
                    g.tensor_tensor(heads(pstate[0:DS], HD), heads(state[0:DS, kc % 2], HD),
                                    tiny[0:DS, 4 + kc % 2, NH:2 * NH].unsqueeze(2).broadcast_to([DS, NH, HD]), ALU.mult).then_inc(S["ps_ready"], 1)
                if ok[3]:
                    wait(pool, "ssq_ready", s_ - 3)
                    wait(pool, "out_done", s_ - 4)
                    link(g.tensor_tensor(tiny[:, 6, 0:1], tiny[:, 6, 1:2], consts[:, 3, 0:1], ALU.add))
                    g.tensor_tensor(tiny[:, 6, 2:3], tiny[:, 6, 0:1], consts[:, 0, 0:1], ALU.pow).then_inc(S["rs_ready"], 1)
                if ok[1]:
                    kc = (k - 2) % SLOTS
                    wait(pool, "dt_ready", s_ - 1)
                    wait(pool, "p_cum", s_ - 2)
                    g.tensor_tensor(dam, upto.unsqueeze(1).broadcast_to([P, NH, P]),
                                    tiny[:, 2 + kc % 2, NH:2 * NH].unsqueeze(2).broadcast_to([P, NH, P]), ALU.mult).then_inc(S["dam_ready"], 1)
                end_chain()

            pool.wait_ge(S["w_done"], 1)
            schedule(g, slot)

        @block.vector
        def _(dve):
            v = nc.vector
            for t in range(NT):
                if t % TPC == 0:
                    dve.wait_ge(S[f"x_in{t // TPC}"], 16)
                v.bn_stats(stats[:, t, :], xn[:, t, :]).then_inc(S["vch"], 1)
            for t in range(NT):
                dve.wait_ge(S["vch"], t + 1)
                last = v.bn_aggr(mv[:, t, :], stats[:, t, :])
            last.then_inc(S["stats_done"], 1)
            dve.wait_ge(S["rstd_done"], 1)
            for t in range(NT):
                last = v.tensor_scalar(xn[:, t, :], xn[:, t, :], mv[:, t, 0:1], rstd[:, t:t + 1], ALU.subtract, ALU.mult)
                last.then_inc(S["norm_done"], 1)
            dve.wait_ge(S["small_in"], 32)
            dve.wait_ge(S["const_ready"], 1)
            v.tensor_scalar(a1_wide[:], ones[:], a_col[:, 0:1], None, ALU.mult).then_inc(S["a1_ready"], 1)
            dve.wait_ge(S["fcol_done"], 1)
            v.tensor_copy(fcol[:], ps[0][:, 0:2 * NT].rearrange("p (t c) -> p t c", c=2)).then_inc(S["f2_copied"], 1)
            dve.wait_ge(S["f2_copied"], 1)
            v.tensor_scalar(neg_f2[:], fcol[:, :, 1], -1.0, None, ALU.mult).then_inc(S["f2_copied"], 1)
            v.tensor_reduce(grow[:, 5:6], fcol[:, :, 1], AX_X, ALU.max).then_inc(S["fmax_done"], 1)
            for c in range(8):
                dve.wait_ge(S["f1_done"], c + 1)
                v.tensor_copy(f1_rows[:, c * 512:(c + 1) * 512], ps[1 + c % 2][:, :]).then_inc(S["f1_copied"], 1)
            dve.wait_ge(S["shift_done"], 1)
            v.tensor_scalar(hcol[:, 0], fcol[:, :, 0], grow[:, 6:7], 1.0 - SLOPE, ALU.add, ALU.mult).then_inc(S["vch"], 1)
            v.tensor_scalar(hcol[:, 1], fcol[:, :, 0], grow[:, 6:7], SLOPE - 1.0, ALU.add, ALU.mult).then_inc(S["vch"], 1)
            v.tensor_scalar(grow[:, 7:8], grow[:, 6:7], -1.0, SHIFT, ALU.mult, ALU.add).then_inc(S["vch"], 1)
            dve.wait_ge(S["vch"], NT + 3)
            v.tensor_scalar(hcol[:, 0], hcol[:, 0], 0.0, -SHIFT, ALU.min, ALU.add)
            v.tensor_scalar(hcol[:, 1], hcol[:, 1], 0.0, None, ALU.min)
            v.tensor_scalar(grow[:, 5:6], grow[:, 6:7], -SLOPE, None, ALU.mult).then_inc(S["roww_done"], 1)
            dve.wait_ge(S["colw_done"], 1)
            v.tensor_tensor(colw[:, :, :, 1], colw[:, :, :, 0], colw[:, :, :, 0], ALU.mult).then_inc(S["colw_done"], 1)
            dve.wait_ge(S["ysum_done"], 1)
            v.tensor_scalar(col_mean[:], ps[3][:, 0:F], 1.0 / N, None, ALU.mult).then_inc(S["colmean_done"], 1)
            dve.wait_ge(S["colw_done"], 2)

            def build_y(first, names):
                prod, hi, done = (S[n] for n in names)
                cols = XC if first else F
                for q in range(NB):
                    for s in range(2):
                        n = q * 2 + s
                        if not first and s == 0:
                            dve.wait_ge(S["mm_done"], R1 - NB + q + 1)
                            dve.wait_ge(S["feat_done"], (q + 1) * JB)
                        w = ywork[:, (n % 2) * JB * XC:(n % 2 + 1) * JB * XC].rearrange("p (t c) -> p t c", c=XC)
                        t0 = q * JB
                        if n >= 2:
                            dve.wait_ge(done, n - 1)
                        if first:
                            v.tensor_copy(w[:, :, F:XC], colw[:, s, t0:t0 + JB, :])
                        v.tensor_tensor(w[:, :, 0:F], xn[:, t0:t0 + JB, :],
                                        colw[:, s, t0:t0 + JB, 0:1].broadcast_to([P, JB, F]), ALU.mult).then_inc(prod, 1)
                        if n >= 1:
                            low(n - 1, cols, hi, done)
                low(2 * NB - 1, cols, hi, done)

            def low(n, cols, hi, done):
                q, s = n // 2, n % 2
                w = ywork[:, (n % 2) * JB * XC:(n % 2 + 1) * JB * XC].rearrange("p (t c) -> p t c", c=XC)
                dve.wait_ge(hi, n + 1)
                v.tensor_tensor(Y[:, q * JB:(q + 1) * JB, s, 1, 0:cols], w[:, :, 0:cols],
                                Y[:, q * JB:(q + 1) * JB, s, 0, 0:cols].bitcast(F32), ALU.subtract).then_inc(done, 1)

            build_y(True, ("y_prod", "y_hi", "y_done"))

            def codes(G, par, jt, first=False):
                n = G * NT + jt
                dve.wait_ge(S["tr_done"], n + 1)
                rows = bass.ds(v.snap(G * 512) if not isinstance(G, int) else G * 512, 512)
                v.scalar_tensor_tensor(
                    out=code[:, par, :, jt * P:(jt + 1) * P], in0=f1_rows[:, rows].rearrange("p (i r) -> p i r", i=IT),
                    scalar=neg_f2[:, jt:jt + 1], in1=ps[jt % TRB][:, :].rearrange("p (i r) -> p i r", i=IT),
                    op0=ALU.is_gt, op1=ALU.add).then_inc(S["coded"], 1)

            def mask_c(n, src, b):
                wait(dve, "mm_done", n - (MASKS - 1))
                v.tensor_scalar(maskC[:, b % MASKS], src, 2.0, None, ALU.is_equal).then_inc(S["maskC_ready"], 1)

            def mask1(G, par, b):
                if b >= BLOCKS:
                    G, par, b = G + 1, 1 - par, b - BLOCKS
                it, ch = b // NB, b % NB
                dve.wait_ge(S["coded"], G * NT + (NT if it else (ch + 1) * JB))
                mask_c(G * BLOCKS + b, code[:, par, it, ch * JB * P:(ch + 1) * JB * P], b)

            def sum1(T, k):
                row = v.snap(T) if not isinstance(T, int) else T
                w = roww[:, bass.ds(row, 1), 1:2].rearrange("p a b -> p (a b)")
                dve.wait_ge(S["acc_read"], T + 1)
                wait(dve, "scaled_done", T - 1)
                both = accC[k][:, 0:2 * XC].rearrange("p (a b) -> p a b", a=2)
                v.tensor_scalar(q_c[:, k], both[:, :, F + 1], w, w, ALU.mult, ALU.mult)
                v.scalar_tensor_tensor(out=ps_sum[:, k], in0=both, scalar=w, in1=acc_s[:, k], op0=ALU.mult, op1=ALU.add).then_inc(S["summed"], 1)

            def feat1(T, k):
                row = v.snap(T) if not isinstance(T, int) else T
                mine = xn[:, bass.ds(row, 1), :].rearrange("p a b -> p (a b)")
                dve.wait_ge(S["scaled_done"], T + 1)
                link(v.scalar_tensor_tensor(out=fwork[:, 0], in0=mine, scalar=k_one[:, k], in1=scaled[:, k], op0=ALU.mult, op1=ALU.add))
                link(v.tensor_scalar(fwork[:, 1], fwork[:, 0], -THRESH, THRESH, ALU.max, ALU.min))
                v.tensor_tensor(mine, fwork[:, 0], fwork[:, 1], ALU.subtract).then_inc(S["feat_done"], 1)
                end_chain()

            def supertile(G, par, first=False, last=False):
                for b in range(BLOCKS):
                    it, ch = b // NB, b % NB
                    if not (last and b + LEAD >= BLOCKS):
                        mask1(G, par, b + LEAD)
                    if not last:
                        if b == 0:
                            wait(dve, "maskA_ready", G * BLOCKS)
                            wait(dve, "spilled", G * 16)
                        for j in range(JH):
                            codes(G + 1, 1 - par, b * JH + j)
                    if ch == 2 and not (first and it < 1):
                        sum1(G * IT + (it - 1), (it - 1) % 2)
                    if ch == 0 and not (first and it < 2):
                        feat1(G * IT + (it - 2), it % 2)

            chain = [0]

            def step(ins):
                chain[0] += 1
                ins.then_inc(S["vch"], 1)
                return chain[0]

            def link(ins):
                dve.wait_ge(S["vch"], step(ins))

            def end_chain():
                if chain[0]:
                    dve.wait_ge(S["vch"], chain[0])
                    v.sem_clear(S["vch"])
                chain[0] = 0

            chain[0] = NT + 3
            end_chain()
            for jt in range(NT):
                codes(0, 0, jt)
            for b in range(LEAD):
                mask1(0, 0, b)
            supertile(0, 0, first=True)
            with v.Fori(0, NG // 2 - 1) as u:
                supertile(u * 2 + 1, 1)
                supertile(u * 2 + 2, 0)
            supertile(NG - 1, 1, last=True)
            feat1(NT - 2, 0)
            sum1(NT - 1, 1)
            feat1(NT - 1, 1)

            build_y(False, ("y2_prod", "y2_hi", "y2_done"))

            dve.wait_ge(S["w_in"], 16 * 12)
            v.tensor_scalar(w_zdt[:, 0:DI], w_zdt[:, 0:DI], 0.5, None, ALU.mult)
            v.tensor_scalar(conv_wt, conv_wt, 0.5, None, ALU.mult)
            v.tensor_scalar(conv_bt, conv_bt, 0.5, None, ALU.mult).then_inc(S["w_ready"], 1)
            dve.wait_ge(S["w_turned"], 1)
            v.tensor_copy(w_outT, ps[1][:, 0:KB * P].rearrange("p (k n) -> p k n", k=KB)).then_inc(S["w_copied"], 1)
            dve.wait_ge(S["w_mult"], 1)
            for kb in range(KB):
                v.tensor_scalar(w_comb[:, kb], ps[2][:, kb * P:(kb + 1) * P], normw[:, kb:kb + 1], float(np.sqrt(DI)), ALU.mult, ALU.mult)
            dve.wait_ge(S["w_ready"], 2)
            v.tensor_scalar(a_row, a_row, -1.0, None, ALU.mult).then_inc(S["w_done"], 1)

            def series(z):
                root = np.sqrt(z)
                return np.where(z > 1e-8, 2 * np.arctanh(root) / np.maximum(root, 1e-9), 2 + 2 * z / 3)

            top = 1.0 / 9.0
            points = top / 2 * (1 - np.cos(np.pi * (np.arange(64) + 0.5) / 64))
            log_c = [float(c) for c in np.polynomial.Polynomial.fit(points, series(points), 5, domain=[0, top]).convert().coef]

            def mask2(n, k, j):
                b = j % NB
                dve.wait_ge(S[f"codes_in{k}"], code_count(n, k, b))
                mask_c(n + R1, code[:, 0, k, b * JB * P:(b + 1) * JB * P], b)

            def heads(ap):
                return ap.rearrange("p (h w) -> p h w", h=NH)

            def slot(s_, k, now, then, ok):
                def mask(j):
                    if (now if j + LEAD < NB else then):
                        mask2(s_ * NB + (j + LEAD), (k + (j + LEAD) // NB) % SLOTS, j + LEAD)

                mask(0)
                if ok[3]:
                    kc = k % 2
                    dve.wait_ge(S["p_y"], s_ - 3)
                    dve.wait_ge(S["xD_ready"], s_ - 3)
                    dve.wait_ge(S["ps_ready"], s_ - 3)
                    link(v.tensor_tensor(heads(ysum), heads(ps[0][:, DI:2 * DI]),
                                         tiny[:, 4 + kc, 0:NH].unsqueeze(2).broadcast_to([P, NH, HD]), ALU.mult))
                    link(v.tensor_tensor(ysum, ysum, xD, ALU.add))
                    v.tensor_tensor(ysum, ysum, ps[0][:, 0:DI], ALU.add).then_inc(S["y_read"], 1)
                    v.tensor_tensor(state[0:DS, 1 - kc], pstate[0:DS], ps[1][0:DS, 0:DI], ALU.add).then_inc(S["st_done"], 1)
                    dve.wait_ge(S["y_read"], s_ - 3)
                    wait(dve, "p_yT", s_ - 4)
                    wait(dve, "ssq_ready", s_ - 4)
                    v.tensor_tensor(yg, ysum, gate[:, kc], ALU.mult).then_inc(S["yg_ready"], 1)
                if ok[0]:
                    T, kt = s_ - 1, (k - 1) % 2
                    row = v.snap(T) if not isinstance(T, int) else T
                    dve.wait_ge(S["acc_read"], T + (NT + 1))
                    dve.wait_ge(S["base_done"], T + 1)
                    part = sum2.rearrange("p (a b) -> p a b", a=2)
                    done = step(v.scalar_tensor_tensor(
                        out=part, in0=accC[kt][:, 0:2 * F].rearrange("p (a b) -> p a b", a=2),
                        scalar=roww[:, bass.ds(row, 1), 1:2].rearrange("p a b -> p (a b)"), in1=acc_s[:, kt, :, 0:F], op0=ALU.mult, op1=ALU.add))
                    dve.wait_ge(S["vch"], done)
                    link(v.tensor_tensor(part[:, 0], part[:, 0], part[:, 1], ALU.add))
                    wait(dve, "x1b_done", T - 1)
                    v.scalar_tensor_tensor(out=x1[:, kt], in0=part[:, 0], scalar=small[:, 14 + kt:15 + kt], in1=base[:, kt],
                                           op0=ALU.mult, op1=ALU.add).then_inc(S["x1_done"], 1)
                    dve.wait_ge(S["x1_done"], T + 1)
                    link(v.bn_stats(tiny[:, 7, 0:6], x1[:, kt]))
                    v.bn_aggr(tiny[:, 0, 0:2], tiny[:, 7, 0:6]).then_inc(S["ln_done"], 1)
                mask(1)
                if ok[1]:
                    kc = k % 2
                    dve.wait_ge(S["in_read"], s_ - 1)
                    wait(dve, "ew_ready", s_ - 2)
                    link(v.tensor_tensor(tiny[:, 8, 0:NH], zdt[:, DI:DI + NH], dt_b, ALU.add))
                    v.scalar_tensor_tensor(out=tiny[:, 9, 0:NH], in0=tiny[:, 8, 0:NH], scalar=-1.0, in1=tiny[:, 8, 0:NH], op0=ALU.mult, op1=ALU.min).then_inc(S["nv_ready"], 1)
                    dve.wait_ge(S["halo_done"], s_ - 1)
                    wait(dve, "ctan_ready", s_ - 2)
                    wait(dve, "conv_ready", s_ - 2)
                    for cb in range(CB):
                        c0 = step(v.tensor_scalar(conv[:, cb], hist[:, kc, cb, 0:P], conv_wt[:, cb, 0:1], conv_bt[:, cb:cb + 1], ALU.mult, ALU.add))
                    for tap in range(1, TAPS):
                        for cb in range(CB):
                            dve.wait_ge(S["vch"], c0 - (CB - 1))
                            ins = v.scalar_tensor_tensor(out=conv[:, cb], in0=hist[:, kc, cb, tap:tap + P], scalar=conv_wt[:, cb, tap:tap + 1],
                                                         in1=conv[:, cb], op0=ALU.mult, op1=ALU.add)
                            if tap == TAPS - 1 and cb == CB - 1:
                                ins.then_inc(S["conv_pre"], 1)
                            else:
                                c0 = step(ins)
                    dve.wait_ge(S["ew_ready"], s_ - 1)
                    e, two, si, z, p = (tiny[:, i, 0:NH] for i in (10, 11, 12, 13, 14))
                    link(v.tensor_scalar(two, e, 2.0, None, ALU.add))
                    link(v.reciprocal(two, two))
                    link(v.tensor_tensor(si, e, two, ALU.mult))
                    link(v.tensor_tensor(z, si, si, ALU.mult))
                    link(v.tensor_scalar(p, z, log_c[-1], None, ALU.mult))
                    for cf in log_c[-2:0:-1]:
                        link(v.scalar_tensor_tensor(out=p, in0=p, scalar=cf, in1=z, op0=ALU.add, op1=ALU.mult))
                    link(v.scalar_tensor_tensor(out=p, in0=p, scalar=log_c[0], in1=si, op0=ALU.add, op1=ALU.mult))
                    wait(dve, "xdt_ready", s_ - 4)
                    link(v.scalar_tensor_tensor(out=tiny[:, 2 + kc, 0:NH], in0=tiny[:, 8, 0:NH], scalar=0.0, in1=p, op0=ALU.max, op1=ALU.add))
                    v.tensor_tensor(tiny[:, 2 + kc, NH:2 * NH], tiny[:, 2 + kc, 0:NH], a_row, ALU.mult).then_inc(S["dt_ready"], 1)
                mask(2)
                if ok[2]:
                    dve.wait_ge(S["p_g"], s_ - 2)
                    link(v.tensor_tensor(gm, ps[0][:, 0:P], upto, ALU.mult))
                    dve.wait_ge(S["exp_done"], s_ - 2)
                    wait(dve, "p_y", s_ - 3)
                    v.tensor_tensor(wmix, expD, gm.unsqueeze(1).broadcast_to([P, NH, P]), ALU.mult).then_inc(S["mix_ready"], 1)
                if ok[1]:
                    kc = k % 2
                    dve.wait_ge(S["zt_ready"], s_ - 1)
                    v.scalar_tensor_tensor(out=gate[:, kc], in0=ztan, scalar=1.0, in1=zdt[:, 0:DI], op0=ALU.add, op1=ALU.mult).then_inc(S["gate_done"], 1)
                    dve.wait_ge(S["ctan_ready"], s_ - 1)
                    v.scalar_tensor_tensor(out=xbc[:, kc], in0=gate_t, scalar=1.0, in1=conv, op0=ALU.add, op1=ALU.mult).then_inc(S["conv_ready"], 1)
                if ok[0]:
                    kt = (k - 1) % 2
                    dve.wait_ge(S["rstd2"], s_)
                    wait(dve, "p_xT", s_ - 2)
                    v.tensor_scalar(xn2[:, kt], x1[:, kt], tiny[:, 0, 0:1], tiny[:, 1, 1:2], ALU.subtract, ALU.mult).then_inc(S["xn2_ready"], 1)
                mask(3)
                if isinstance(s_, int) and s_ == 0:
                    dve.wait_ge(S["ysum_done"], 2)
                    v.tensor_scalar(col_mean[:], ps[3][:, 0:F], 1.0 / N, None, ALU.mult).then_inc(S["colmean_done"], 1)
                if ok[3]:
                    kc = k % 2
                    dve.wait_ge(S["p_o"], s_ - 3)
                    dve.wait_ge(S["rs_ready"], s_ - 3)
                    wait(dve, f"stored{kc}", (s_ - 4 - kc) * 8)
                    v.scalar_tensor_tensor(out=outb[:, kc], in0=ps[1][:, 0:F], scalar=tiny[:, 6, 2:3], in1=x1b[:, k],
                                           op0=ALU.mult, op1=ALU.add).then_inc(S["out_done"], 1)
                end_chain()

            for b in range(LEAD):
                mask2(b, 0, b)
            schedule(v, slot)

        @block.scalar
        def _(act):
            s = nc.scalar
            s.preload_act_table_set("exp_and_others")
            act.wait_ge(S["small_in"], 32)
            s.activation(grow[:, 0:5], grow[:, 0:5], ACT.Exp, scale=-1.0).then_inc(S["coef_done"], 1)
            for q in range(NT // 4):
                act.wait_ge(S["xT_done"], q + 1)
                s.copy(xnT[:, q * 512:(q + 1) * 512], accA[q % 2][:, :]).then_inc(S["xT_copied"], 1)
            act.wait_ge(S["roww_done"], 1)
            s.activation(roww[:, :, 0], hcol[:, 0], ACT.Exp)
            s.activation(roww[:, :, 1], hcol[:, 1], ACT.Exp).then_inc(S["roww_done"], 1)
            s.activation(colw[:, 0, :, 0], fcol[:, :, 1], ACT.Exp, bias=grow[:, 7:8])
            s.activation(colw[:, 1, :, 0], fcol[:, :, 1], ACT.Exp, bias=grow[:, 5:6], scale=SLOPE).then_inc(S["colw_done"], 1)

            def high_parts(names, cols):
                prod, hi = (S[n] for n in names)
                for n in range(2 * NB):
                    q, sd = n // 2, n % 2
                    w = ywork[:, (n % 2) * JB * XC:(n % 2 + 1) * JB * XC].rearrange("p (t c) -> p t c", c=XC)
                    act.wait_ge(prod, n + 1)
                    s.copy(Y[:, q * JB:(q + 1) * JB, sd, 0, 0:cols], w[:, :, 0:cols]).then_inc(hi, 1)

            high_parts(("y_prod", "y_hi"), XC)

            def sign(G, h, first=False):
                n = G * BLOCKS + h
                c = h // 2
                act.wait_ge(S[f"adj_in{c % 2}"], (G * 4 + (c // 2 + 1)) * 16)
                if not first:
                    act.wait_ge(S["tr_done"], n * 2 - 6)
                s.activation(edges[:, h % 4], adj_in[:, c % 2, :, (h % 2) * 2 * P:(h % 2 + 1) * 2 * P], ACT.Sign).then_inc(S["signed"], 1)

            def mask_a(n, src, b):
                wait(act, "mm_done", n - (MASKS - 1))
                s.activation(maskA[:, b % MASKS], src, ACT.Relu, bias=-2.0).then_inc(S["maskA_ready"], 1)

            def mask1(G, par, b):
                if b >= BLOCKS:
                    G, par, b = G + 1, 1 - par, b - BLOCKS
                it, ch = b // NB, b % NB
                act.wait_ge(S["coded"], G * NT + (NT if it else (ch + 1) * JB))
                mask_a(G * BLOCKS + b, code[:, par, it, ch * JB * P:(ch + 1) * JB * P], b)

            def read_acc(T, k, cols, round_two=0):
                row = s.snap(T) if not isinstance(T, int) else T
                act.wait_ge(S["mm_done"], T * NB + (NB + round_two * R1))
                if round_two:
                    wait(act, "x1_done", T - 1)
                else:
                    wait(act, "scaled_done", T - 1)
                w = roww[:, bass.ds(row, 1), 0:1].rearrange("p a b -> p (a b)")
                src = accA[k][:, 0:2 * cols].rearrange("p (a b) -> p a b", a=2)
                s.mul(acc_s[:, k, :, 0:cols], src, w).then_inc(S["acc_read"], 1)

            def supertile(G, par, first=False, last=False):
                for b in range(BLOCKS):
                    it, ch = b // NB, b % NB
                    if not (last and b + LEAD >= BLOCKS):
                        mask1(G, par, b + LEAD)
                    if not last:
                        sign(G + 1, b)
                    if ch == 1 and not (first and it == 0):
                        read_acc(G * IT + (it - 1), (it - 1) % 2, XC)

            for h in range(BLOCKS):
                sign(0, h, first=h < 4)
            for b in range(LEAD):
                mask1(0, 0, b)
            supertile(0, 0, first=True)
            with s.Fori(0, NG // 2 - 1) as u:
                supertile(u * 2 + 1, 1)
                supertile(u * 2 + 2, 0)
            supertile(NG - 1, 1, last=True)
            read_acc(NT - 1, 1, XC)
            high_parts(("y2_prod", "y2_hi"), F)
            act.wait_ge(S["w_in"], 16 * 12)
            s.activation(a_row, a_row, ACT.Exp).then_inc(S["w_ready"], 1)

            def mask2(n, k, j):
                b = j % NB
                act.wait_ge(S[f"codes_in{k}"], code_count(n, k, b))
                mask_a(n + R1, code[:, 0, k, b * JB * P:(b + 1) * JB * P], b)

            def slot(s_, k, now, then, ok):
                def mask(j):
                    if (now if j + LEAD < NB else then):
                        mask2(s_ * NB + (j + LEAD), (k + (j + LEAD) // NB) % SLOTS, j + LEAD)

                mask(0)
                if ok[0]:
                    read_acc(s_ - 1, (k - 1) % 2, F, 1)
                if ok[1]:
                    act.wait_ge(S["p_xT"], s_ - 1)
                    wait(act, "p_in", s_ - 2)
                    s.copy(xn2T, ps[0][:, 0:P]).then_inc(S["xT_ready"], 1)
                if ok[2]:
                    kc = (k - 3) % 2
                    act.wait_ge(S["p_cum"], s_ - 2)
                    wait(act, "y_read", s_ - 4)
                    wait(act, "ps_ready", s_ - 4)
                    s.activation(tiny[:, 4 + kc, :], ps[2][:, 0:2 * NH], ACT.Exp)
                    wait(act, "mix_ready", s_ - 3)
                    wait(act, "xdt_ready", s_ - 3)
                    s.activation(expD, ps[3][:, 0:NH * P].rearrange("p (h w) -> p h w", h=NH), ACT.Exp).then_inc(S["exp_done"], 1)
                    act.wait_ge(S["p_tr"], s_ - 2)
                    wait(act, "p_y", s_ - 3)
                    wait(act, "xD_ready", s_ - 3)
                    s.copy(xl, ps[1][:, 0:CB * P]).then_inc(S["xl_ready"], 1)
                mask(1)
                if ok[1]:
                    kc = k % 2
                    act.wait_ge(S["p_in"], s_ - 1)
                    wait(act, "dt_ready", s_ - 2)
                    wait(act, "gate_done", s_ - 2)
                    s.copy(zdt, ps[2][:, 0:DI + NH]).then_inc(S["zcopy"], 1)
                    wait(act, "conv_pre", s_ - 3)
                    s.copy(hist[:, kc, :, TAPS - 1:], ps[3][:, 0:CB * P].rearrange("p (c w) -> p c w", c=CB)).then_inc(S["in_read"], 1)
                    act.wait_ge(S["zcopy"], s_ - 1)
                    s.activation(ztan, zdt[:, 0:DI], ACT.Tanh).then_inc(S["zt_ready"], 1)
                    act.wait_ge(S["in_read"], s_ - 1)
                    wait(act, "conv_pre", s_ - 2)
                    s.copy(hist[:, 1 - kc, :, 0:TAPS - 1], hist[:, kc, :, P:P + TAPS - 1]).then_inc(S["halo_done"], 1)
                if ok[2]:
                    act.wait_ge(S["p_ct"], s_ - 2)
                    s.copy(cT[0:DS], ps[0][0:DS, 0:P]).then_inc(S["cT_ready"], 1)
                if ok[3]:
                    act.wait_ge(S["p_yT"], s_ - 3)
                    wait(act, "p_o", s_ - 4)
                    s.copy(yT, ps[1][:, 0:DI].rearrange("p (c w) -> p c w", c=KB)).then_inc(S["yT_ready"], 1)
                    wait(act, "rs_ready", s_ - 4)
                    act.wait_ge(S["yg_ready"], s_ - 3)
                    wait(act, "ssq_ready", s_ - 4)
                    s.activation(junk, yg, ACT.Square, accum_out=tiny[:, 6, 1:2]).then_inc(S["ssq_ready"], 1)
                mask(2)
                if ok[1]:
                    act.wait_ge(S["nv_ready"], s_ - 1)
                    wait(act, "dt_ready", s_ - 2)
                    s.activation(tiny[:, 10, 0:NH], tiny[:, 9, 0:NH], ACT.Exp).then_inc(S["ew_ready"], 1)
                    act.wait_ge(S["conv_pre"], s_ - 1)
                    wait(act, "conv_ready", s_ - 2)
                    s.activation(gate_t, conv, ACT.Tanh).then_inc(S["ctan_ready"], 1)
                mask(3)

            for b in range(LEAD):
                mask2(b, 0, b)
            schedule(s, slot)

        @block.tensor
        def _(pe):
            t_ = nc.tensor
            pe.wait_ge(S["const_ready"], 1)
            for t in range(NT):
                q = t // 4
                if t % 4 == 0 and q >= 2:
                    pe.wait_ge(S["xT_copied"], q - 1)
                pe.wait_ge(S["norm_done"], t + 1)
                m = t_.transpose(accA[q % 2][:, (t % 4) * P:(t % 4 + 1) * P], xn[:, t, :], ident[:])
                if t % 4 == 3:
                    m.then_inc(S["xT_done"], 1)
            pe.wait_ge(S["small_in"], 32)
            for t in range(NT):
                if t % 4 == 0:
                    pe.wait_ge(S["xT_copied"], t // 4 + 1)
                m = t_.matmul(ps[0][:, 2 * t:2 * t + 2], xnT[:, t * P:(t + 1) * P], a_col[:, 0:2], start=True, stop=True)
            m.then_inc(S["fcol_done"], 1)
            pe.wait_ge(S["a1_ready"], 1)
            for c in range(8):
                if c >= 2:
                    pe.wait_ge(S["f1_copied"], c - 1)
                t_.matmul(ps[1 + c % 2][:, :], a1_wide[:], xnT[:, c * 512:(c + 1) * 512], start=True, stop=True).then_inc(S["f1_done"], 1)

            def column_sums():
                for t in range(NT):
                    m = t_.matmul(ps[3][:, 0:F], ones[:], xn[:, t, :], start=t == 0, stop=t == NT - 1)
                m.then_inc(S["ysum_done"], 1)

            column_sums()

            def turn(G, b, first=False):
                pe.wait_ge(S["signed"], G * BLOCKS + b + 1)
                for j in range(JH):
                    jt = b * JH + j
                    if not (first and jt < TRB):
                        pe.wait_ge(S["coded"], G * NT + (jt - TRB + 1))
                    for it in range(IT):
                        m = t_.matmul(ps[jt % TRB][:, it * P:(it + 1) * P], edges[:, b % 4, it, j * P:(j + 1) * P], ident2[:], start=True, stop=True)
                    m.then_inc(S["tr_done"], 1)

            def products(n, k, b, ch, cols, y=None):
                pe.wait_ge(S["maskA_ready"], n + 1)
                if y is not None:
                    pe.wait_ge(y, 2 * ch + 2)
                for l in range(JB):
                    jt = ch * JB + l
                    t_.matmul(accA[k][:, 0:2 * cols], maskA[:, b % MASKS, l * P:(l + 1) * P], Y[:, jt, 0, :, 0:cols],
                              start=jt == 0, stop=jt == NT - 1)
                pe.wait_ge(S["maskC_ready"], n + 1)
                for l in range(JB):
                    jt = ch * JB + l
                    m = t_.matmul(accC[k][:, 0:2 * cols], maskC[:, b % MASKS, l * P:(l + 1) * P], Y[:, jt, 1, :, 0:cols],
                                  start=jt == 0, stop=jt == NT - 1)
                m.then_inc(S["mm_done"], 1)

            def supertile(G, par, first=False, last=False):
                for b in range(BLOCKS):
                    it, ch = b // NB, b % NB
                    if ch == 0 and not (first and it < 2):
                        free_acc(G * IT + (it - 2))
                    products(G * BLOCKS + b, it % 2, b, ch, XC, S["y_done"] if first and it == 0 else None)
                    if not last:
                        turn(G + 1, b)

            def free_acc(T):
                pe.wait_ge(S["acc_read"], T + 1)
                pe.wait_ge(S["summed"], T + 1)

            for b in range(BLOCKS):
                turn(0, b, first=True)
            supertile(0, 0, first=True)
            with t_.Fori(0, NG // 2 - 1) as u:
                supertile(u * 2 + 1, 1)
                supertile(u * 2 + 2, 0)
            supertile(NG - 1, 1, last=True)
            free_acc(NT - 1)

            def weights():
                pe.wait_ge(S["w_in"], 16 * 12)
                for kb in range(KB):
                    m = t_.transpose(ps[1][:, kb * P:(kb + 1) * P], w_out[:, kb], ident[:])
                m.then_inc(S["w_turned"], 1)
                pe.wait_ge(S["w_copied"], 1)
                for kb in range(KB):
                    m = t_.matmul(ps[2][:, kb * P:(kb + 1) * P], w_outT[:, kb], w_lin, start=True, stop=True)
                m.then_inc(S["w_mult"], 1)

            weights()

            def slot(s_, k, now, then, ok):
                def block(ch):
                    if now:
                        if ch == 0:
                            wait(pe, "acc_read", s_ + (NT - 1))
                            wait(pe, "x1_done", s_ - 1)
                        early = isinstance(s_, int) and s_ == 0
                        products(s_ * NB + (R1 + ch), k % 2, ch, ch, F, S["y2_done"] if early else None)
                        if early and ch == 2:
                            column_sums()

                c = k % 2
                if ok[1]:
                    pe.wait_ge(S["xn2_ready"], s_ - 1)
                    if ok[3]:
                        pe.wait_ge(S["y_read"], s_ - 3)
                    t_.transpose(ps[0][:, 0:P], xn2[:, c], ident[:]).then_inc(S["p_xT"], 1)
                if ok[2]:
                    c3 = (k - 3) % 2
                    da = tiny[:, 2 + c3, NH:2 * NH]
                    pe.wait_ge(S["dam_ready"], s_ - 2)
                    pe.wait_ge(S["in_read"], s_ - 2)
                    pe.wait_ge(S["conv_ready"], s_ - 2)
                    t_.matmul(ps[2][:, 0:NH], upto, da, start=True, stop=True)
                    t_.matmul(ps[2][:, NH:2 * NH], ones[:], da, start=True, stop=True)
                    t_.matmul(ps[3][:, 0:NH * P], after, dam.rearrange("p h w -> p (h w)"), start=True, stop=True).then_inc(S["p_cum"], 1)
                    if ok[3]:
                        pe.wait_ge(S["st_done"], s_ - 3)
                    for cb in range(CB):
                        m = t_.transpose(ps[1][:, cb * P:(cb + 1) * P], xbc[:, c3, cb], ident[:])
                    m.then_inc(S["p_tr"], 1)
                block(0)
                if ok[1]:
                    pe.wait_ge(S["xT_ready"], s_ - 1)
                    if ok[2]:
                        pe.wait_ge(S["exp_done"], s_ - 2)
                    t_.matmul(ps[2][:, 0:DI + NH], xn2T, w_zdt, start=True, stop=True)
                    for cb in range(CB):
                        m = t_.matmul(ps[3][:, cb * P:(cb + 1) * P], w_xbc[:, cb * P:(cb + 1) * P], xn2T, start=True, stop=True)
                    m.then_inc(S["p_in"], 1)
                if ok[2]:
                    pe.wait_ge(S["xl_ready"], s_ - 2)
                    t_.matmul(ps[0][0:DS, 0:P], xl[:, DI + DS:DI + 2 * DS], ident[:], start=True, stop=True).then_inc(S["p_ct"], 1)
                if ok[3]:
                    pe.wait_ge(S["yg_ready"], s_ - 3)
                    for kb in range(KB):
                        m = t_.transpose(ps[1][:, kb * P:(kb + 1) * P], yg[:, kb * P:(kb + 1) * P], ident[:])
                    m.then_inc(S["p_yT"], 1)
                block(1)
                if ok[2]:
                    pe.wait_ge(S["cT_ready"], s_ - 2)
                    t_.matmul(ps[0][:, 0:P], xbc[0:DS, (k - 3) % 2, CB - 1, :], cT[0:DS], start=True, stop=True).then_inc(S["p_g"], 1)
                if ok[3]:
                    pe.wait_ge(S["yT_ready"], s_ - 3)
                    for kb in range(KB):
                        m = t_.matmul(ps[1][:, 0:F], yT[:, kb], w_comb[:, kb], start=kb == 0, stop=kb == KB - 1)
                    m.then_inc(S["p_o"], 1)
                block(2)
                if ok[2]:
                    c3 = (k - 3) % 2
                    pe.wait_ge(S["mix_ready"], s_ - 2)
                    pe.wait_ge(S["xdt_ready"], s_ - 2)
                    if ok[3]:
                        pe.wait_ge(S["out_done"], s_ - 3)
                    for h in range(NH):
                        t_.matmul(ps[0][:, h * HD:(h + 1) * HD], wmix[:, h], xdt[:, h * HD:(h + 1) * HD], start=True, stop=True)
                    t_.matmul(ps[0][:, DI:2 * DI], cT[0:DS], state[0:DS, c3], start=True, stop=True)
                    t_.matmul(ps[1][0:DS, 0:DI], xl[:, DI:DI + DS], xdtd, start=True, stop=True).then_inc(S["p_y"], 1)
                block(3)

            schedule(t_, slot)


_INS = ['x', 'adj', 'L0_gnn_h0', 'L0_gnn_a', 'L0_gnn_temp', 'L0_ffn_W_in', 'L0_ffn_conv_w', 'L0_ffn_conv_b',
        'L0_ffn_dt_bias', 'L0_ffn_A_log', 'L0_ffn_D', 'L0_ffn_norm_w', 'L0_ffn_W_out', 'L0_ffn_W_lin', 'L0_ffn_b_lin']
_OUTS = [((4096, 128), 'float32')]


def kernel(**inputs):
    import numpy as _np
    import concourse.bacc as _bacc
    from concourse import mybir as _mybir
    from concourse.bass_utils import run_bass_kernel_spmd as _run

    nc = _bacc.Bacc("TRN2", target_bir_lowering=False, num_devices=1)
    arrays, args = {}, []
    for name in _INS:
        arr = _np.ascontiguousarray(inputs[name])
        arrays[f"in_{name}_dram"] = arr
        args.append(nc.dram_tensor(f"in_{name}_dram", arr.shape, _mybir.dt.from_np(arr.dtype), kind="ExternalInput").ap())
    for i, (shape, dtype) in enumerate(_OUTS):
        dt = _mybir.dt.from_np(_np.dtype(dtype))
        args.append(nc.dram_tensor(f"out_{i}_dram", shape, dt, kind="ExternalOutput").ap())
    gnn_ffn_kernel(nc, *args)
    r = _run(nc, [arrays], core_ids=[0])
    return r.results[0]["out_0_dram"]
```

```python
from contextlib import ExitStack

import numpy as np

import concourse.bass as bass
from concourse import mybir

F32 = mybir.dt.float32
F32R = mybir.dt.float32r
BF16 = mybir.dt.bfloat16
I8 = mybir.dt.int8
ALU = mybir.AluOpType
ACT = mybir.ActivationFunctionType
AX_X = mybir.AxisListType.X

P = 128
SHIFT = 30.0
THRESH = 1e-06
EPS = 1e-05
SLOPE = 0.2


def gnn_ffn_kernel(nc, x, adj, h0, a, temp, W_in, conv_w, conv_b, dt_bias, A_log, D, norm_w, W_out, W_lin, b_lin, out):
    N, F = x.shape
    NT = N // P
    IT = 4
    NG = NT // IT
    JB = 8
    NB = NT // JB
    BLOCKS = IT * NB
    JH = NT // BLOCKS
    XC = F + 2
    MASKS = 4
    TRB = 4
    assert F == P and NG % 2 == 0

    x_v = x.rearrange("(t p) f -> p t f", p=P)
    h0_v = h0.rearrange("(t p) f -> t p f", p=P)
    out_v = out.rearrange("(t p) f -> t p f", p=P)
    xt_v = x.rearrange("(t p) f -> t p f", p=P)
    adj_v = adj.rearrange("(g i p) j -> g p i j", i=IT, p=P)
    code_dram = nc.dram_tensor("edge_codes", (NT, P, NT * P), I8, kind="Internal").ap()

    with ExitStack() as ctx:
        def sb(name, shape, dt=F32):
            return ctx.enter_context(nc.sbuf_tensor(name, shape, dt))

        def sem(name):
            return ctx.enter_context(nc.semaphore(name))

        def psum(name, shape, dt=F32):
            return ctx.enter_context(nc.psum_tensor(name, shape, dt))

        adj_in = sb("adj_in", [P, 4, IT, JH * P])
        edges = sb("edges", [P, 4, IT, 2 * P], BF16)
        code = sb("code", [P, 2, IT, NT * P], I8)
        maskA = sb("maskA", [P, MASKS, JB * P], F32R)
        maskC = sb("maskC", [P, MASKS, JB * P], F32R)
        Y = sb("Y", [P, NT, 2, 2, XC], F32R)
        f1_rows = sb("f1_rows", [P, N])
        xn = sb("xn", [P, NT, F])
        xnT = code[:, 1, :, :].rearrange("p i j -> p (i j)").bitcast(F32)
        ywork = sb("ywork", [P, 2 * JB * XC])

        ident = sb("ident", [P, P])
        ident2 = sb("ident2", [P, P], BF16)
        ones = sb("ones", [P, P])
        a_col = sb("a_col", [P, 1])
        a2_row = sb("a2_row", [P, F])
        a1_wide = sb("a1_wide", [P, P])
        col_mean = sb("col_mean", [P, F])
        stats = sb("stats", [P, NT, 6])
        mv = sb("mv", [P, NT, 2])
        rstd = sb("rstd", [P, NT])
        consts = sb("consts", [P, 4, NT])
        fcol = sb("fcol", [P, NT, 2])
        neg_f2 = sb("neg_f2", [P, NT])
        grow = sb("grow", [P, 8])
        colw = sb("colw", [P, 2, NT, 2])
        roww = sb("roww", [P, NT, 2])
        hcol = sb("hcol", [P, 2, NT])
        coef = sb("coef", [P, 12])
        acc_s = sb("acc_s", [P, 2, 2, XC])
        ps_sum = sb("ps_sum", [P, 2, 2, XC])
        q_c = sb("q_c", [P, 2, 2])
        k_one = sb("k_one", [P, 2, 1])
        num = sb("num", [P, XC])
        small = sb("small", [P, 24])
        row_out = sb("row_out", [P, NT, 4])
        featw = sb("featw", [P, 2, F])
        featsum = sb("featsum", [P, F])
        scaled = sb("scaled", [P, 2, F])
        fwork = sb("fwork", [P, 2, F])

        f2_prod = code[:, 0, :, :].rearrange("p i j -> p (i j)").bitcast(F32).rearrange("p (t f) -> p t f", f=F)

        def y_buffer(side):
            return ywork[:, side * JB * XC:(side + 1) * JB * XC].rearrange("p (t c) -> p t c", c=XC)

        class Space:
            def __init__(self, flat):
                self.flat, self.at = flat, 0

            def take(self, *shape):
                n = 1
                for d in shape:
                    n *= d
                assert self.at + n <= self.flat.shape[1], shape
                v = self.flat[:, self.at:self.at + n]
                self.at += n
                if len(shape) == 1:
                    return v
                names = "abcd"[:len(shape)]
                sizes = {names[i]: shape[i] for i in range(len(shape) - 1)}
                return v.rearrange(f"p ({' '.join(names)}) -> p {' '.join(names)}", **sizes)

        rows_space = Space(f1_rows[:, :])
        adj_space = Space(adj_in[:, :, :, :].rearrange("p a b c -> p (a b c)"))
        code_space = Space(code[:, 1, :, :].rearrange("p i j -> p (i j)").bitcast(F32))

        y_space = Space(ywork[:, :])

        DI = W_out.shape[0]
        NH = dt_bias.shape[0]
        HD = DI // NH
        DS = (conv_w.shape[0] - DI) // 2
        TAPS = conv_w.shape[1]
        CB = conv_w.shape[0] // P
        KB = DI // P
        w_zdt = rows_space.take(DI + NH)
        w_xbc = rows_space.take(CB * P)
        w_out = rows_space.take(KB, P)
        w_outT = rows_space.take(KB, P)
        w_lin = rows_space.take(P)
        w_comb = rows_space.take(KB, P)
        conv_wt = rows_space.take(CB, TAPS)
        conv_bt = rows_space.take(CB)
        normw = rows_space.take(KB)
        b_row = rows_space.take(P)
        dt_b = rows_space.take(NH)
        a_row = rows_space.take(NH)
        d_row = rows_space.take(NH)
        upto = rows_space.take(P)
        after = rows_space.take(P)
        x_in = adj_space.take(2, F)
        h0_in = adj_space.take(2, F)
        base = adj_space.take(2, F)
        x1 = adj_space.take(2, F)
        x1b = adj_space.take(4, F)
        xn2 = adj_space.take(2, F)
        xn2T = adj_space.take(F)
        outb = adj_space.take(2, F)
        hist = adj_space.take(2, CB, P + TAPS - 1)
        conv = code_space.take(CB, P)
        gate_t = code_space.take(CB, P)
        xbc = code_space.take(2, CB, P)
        xl = code_space.take(CB * P)
        zdt = code_space.take(DI + NH)
        ztan = y_space.take(DI)
        cT = adj_space.take(P)
        gate = rows_space.take(2, DI)
        dam = rows_space.take(NH, P)
        expD = code_space.take(NH, P)
        gm = adj_space.take(P)
        wmix = code_space.take(NH, P)
        xdt = adj_space.take(DI)
        xdtd = rows_space.take(DI)
        xD = adj_space.take(DI)
        yg = rows_space.take(DI)
        yT = adj_space.take(KB, P)
        state = code_space.take(2, DI)
        pstate = y_space.take(DI)
        ysum = y_space.take(DI)
        junk = y_space.take(DI)
        sum2 = y_space.take(2 * F)
        tiny = rows_space.take(16, 8)

        ps = [psum(f"ps{i}", [P, 512]) for i in range(4)]
        accA = [psum(f"accA{i}", [P, 512]) for i in range(2)]
        accC = [psum(f"accC{i}", [P, 512]) for i in range(2)]

        names = """x_in0 x_in1 x_in2 x_in3 small_in const_ready stats_done rstd_done norm_done xT_done xT_copied
            fcol_done sums_done fcol_copied f2_prod_done f2_copied fmax_done shift_done bias_ready roww_done featsum_done colw_done f1_done f1_copied ysum_done colmean_done coef_done
            a1_ready y_prod y_hi y_done adj_in0 adj_in1 adj_in2 adj_in3 signed tr_done coded maskA_ready maskC_ready mm_done acc_read summed
            spilled scaled_done feat_done pch vch codes_in0 codes_in1 codes_in2 codes_in3 y2_prod y2_prod_pool y2_hi y2_done
            rowx_in0 rowx_in1 base_done x1_done x1b_done stored0 stored1 w_in w_ready w_turned w_copied w_mult w_done
            ln_done rstd2 xn2_ready p_xT p_in p_cum p_ct p_g p_y p_yT p_o xT_ready xl_ready in_read
            zt_ready nv_ready ew_ready dt_ready dam_ready conv_pre ctan_ready conv_ready halo_done gate_done
            cT_ready mix_ready xdt_ready xD_ready ps_ready y_read yg_ready st_done yT_ready ssq_ready rs_ready
            exp_done out_done zcopy""".split()
        S = {n: sem(n) for n in names}
        block = ctx.enter_context(nc.Block())
        R1 = NG * BLOCKS
        LEAD = 2
        SLOTS = 4
        STAGES = 5

        def wait(eng, name, value):
            if not isinstance(value, int) or value > 0:
                eng.wait_ge(S[name], value)

        def code_count(n, k, b):
            return (n - b - k * NB) + 16 if not isinstance(n, int) else (n - b - k * NB) // NB // SLOTS * 16 + 16

        def schedule(eng, slot):
            def fixed(s_):
                slot(s_, s_ % SLOTS, s_ < NT, s_ + 1 < NT, [0 <= s_ - d < NT for d in range(1, STAGES + 1)])

            for s_ in range(2 * SLOTS):
                fixed(s_)
            with eng.Fori(0, NT // SLOTS - 3) as u:
                for k in range(SLOTS):
                    slot(u * SLOTS + (k + 2 * SLOTS), k, True, True, [True] * STAGES)
            for s_ in range(NT - SLOTS, NT + STAGES):
                fixed(s_)

        XCH = 4
        TPC = NT // XCH
        SPILL_AT = 8

        @block.sync
        def _(sp):
            for k in range(XCH):
                sp.dma_start(xn[:, k * TPC:(k + 1) * TPC, :], x_v[:, k * TPC:(k + 1) * TPC, :]).then_inc(S[f"x_in{k}"], 16)
            sp.dma_start(a_col[:], a[0:F]).then_inc(S["small_in"], 16)
            sp.dma_start(a2_row[:], a[F:2 * F].rearrange("f o -> o f").broadcast_to([P, F])).then_inc(S["small_in"], 16)
            sp.dma_start(grow[:, 0:5], temp.rearrange("(o c) -> o c", o=1).broadcast_to([P, 5])).then_inc(S["small_in"], 16)

            def load_adj(G, h, wait=True):
                row = sp.snap(G) if not isinstance(G, int) else G
                if wait:
                    sp.wait_ge(S["signed"], G * BLOCKS + (h - 3))
                src = adj_v[bass.ds(row, 1), :, :, h * JH * P:(h + 1) * JH * P].rearrange("g p i j -> (g p) i j")
                sp.dma_start(adj_in[:, h % 4], src).then_inc(S[f"adj_in{h % 4}"], 16)

            def spill(G, par):
                row = sp.snap(G * IT) if not isinstance(G, int) else G * IT
                sp.wait_ge(S["coded"], (G + 1) * NT)
                dst = code_dram[bass.ds(row, IT)].rearrange("i p j -> p i j")
                sp.dma_start(dst, code[:, par]).then_inc(S["spilled"], 16)

            for h in range(BLOCKS):
                load_adj(0, h, wait=h >= 4)
            for h in range(SPILL_AT):
                load_adj(1, h)
            spill(0, 0)
            for h in range(SPILL_AT, BLOCKS):
                load_adj(1, h)
            with nc.sync.Fori(1, NG // 2) as u:
                for par in range(2):
                    for h in range(SPILL_AT):
                        load_adj(u * 2 + par, h)
                    spill(u * 2 + (par - 1), 1 - par)
                    for h in range(SPILL_AT, BLOCKS):
                        load_adj(u * 2 + par, h)

            def load_codes(T, k):
                row = sp.snap(T) if not isinstance(T, int) else T
                if not isinstance(T, int) or T >= SLOTS:
                    taken = sp.snap((T - SLOTS + 1) * NB + R1) if not isinstance(T, int) else (T - SLOTS + 1) * NB + R1
                    sp.wait_ge(S["maskA_ready"], taken)
                    sp.wait_ge(S["maskC_ready"], taken)
                sp.dma_start(code[:, 0, k, :], code_dram[bass.ds(row, 1)].rearrange("i p j -> (i p) j")).then_inc(S[f"codes_in{k}"], 16)

            sp.wait_ge(S["spilled"], 16 * (NG - 1))
            sp.wait_ge(S["maskA_ready"], R1 - BLOCKS)
            sp.wait_ge(S["maskC_ready"], R1 - BLOCKS)
            for T in range(SLOTS - 1):
                load_codes(T, T)
            spill(NG - 1, 1)

            sp.wait_ge(S["coded"], NG * NT)
            zw = DI + CB * P
            sp.dma_start(w_zdt[:, 0:DI], W_in[:, 0:DI]).then_inc(S["w_in"], 16)
            sp.dma_start(w_zdt[:, DI:DI + NH], W_in[:, zw:zw + NH]).then_inc(S["w_in"], 16)
            sp.dma_start(w_xbc, W_in[:, DI:zw]).then_inc(S["w_in"], 16)
            sp.dma_start(w_out, W_out.rearrange("(k p) n -> p k n", p=P)).then_inc(S["w_in"], 16)
            sp.dma_start(w_lin, W_lin).then_inc(S["w_in"], 16)
            sp.dma_start(conv_wt, conv_w.rearrange("(k p) n -> p k n", p=P)).then_inc(S["w_in"], 16)
            sp.dma_start(conv_bt, conv_b.rearrange("(k p) -> p k", p=P), allow_slow_non_contiguous=True).then_inc(S["w_in"], 16)
            sp.dma_start(normw, norm_w.rearrange("(k p) -> p k", p=P), allow_slow_non_contiguous=True).then_inc(S["w_in"], 16)
            for dst, src, n in ((b_row, b_lin, P), (dt_b, dt_bias, NH), (a_row, A_log, NH), (d_row, D, NH)):
                sp.dma_start(dst, src.rearrange("(o c) -> o c", o=1).broadcast_to([P, n])).then_inc(S["w_in"], 16)

            def load_rows(T, k):
                row = sp.snap(T) if not isinstance(T, int) else T
                wait(sp, "base_done", T - 1)
                sp.dma_start(x_in[:, k], xt_v[bass.ds(row, 1)].rearrange("i p j -> (i p) j")).then_inc(S[f"rowx_in{k}"], 16)
                sp.dma_start(h0_in[:, k], h0_v[bass.ds(row, 1)].rearrange("i p j -> (i p) j")).then_inc(S[f"rowx_in{k}"], 16)

            def store(T, k):
                row = sp.snap(T) if not isinstance(T, int) else T
                sp.wait_ge(S["out_done"], T + 1)
                sp.dma_start(out_v[bass.ds(row, 1)].rearrange("i p j -> (i p) j"), outb[:, k]).then_inc(S[f"stored{k}"], 16)

            sp.wait_ge(S["spilled"], 16 * NG)
            load_rows(0, 0)

            def slot(s_, k, now, then, ok):
                if not isinstance(s_, int) or s_ + SLOTS - 1 < NT:
                    load_codes(s_ + (SLOTS - 1), (k + SLOTS - 1) % SLOTS)
                if then:
                    load_rows(s_ + 1, (k + 1) % 2)
                if ok[4]:
                    store(s_ - 5, (k - 1) % 2)

            schedule(nc.sync, slot)
            sp.wait_ge(S["stored0"], 8 * NT)
            sp.wait_ge(S["stored1"], 8 * NT)

        @block.gpsimd
        def _(pool):
            g = nc.gpsimd
            chain = [0]

            def link(ins):
                chain[0] += 1
                ins.then_inc(S["pch"], 1)
                pool.wait_ge(S["pch"], chain[0])

            def end_chain():
                g.sem_clear(S["pch"])
                chain[0] = 0

            g.memset(consts[:, 0], -0.5)
            g.memset(consts[:, 1], -1.0)
            g.memset(consts[:, 2], EPS)
            g.memset(consts[:, 3], EPS * DI)
            g.memset(ones[:], 1.0)
            g.memset(ident2[:], 0.0)
            link(g.memset(ident[:], 0.0))
            g.affine_select(out=ident2[:], in_=ident2[:], compare_op=ALU.not_equal, fill=2.0, base=0,
                            pattern=[[-1, P]], channel_multiplier=1)
            g.affine_select(out=ident[:], in_=ident[:], compare_op=ALU.not_equal, fill=1.0, base=0,
                            pattern=[[-1, P]], channel_multiplier=1).then_inc(S["const_ready"], 1)
            def f2_product(k):
                mine = slice(k * TPC, (k + 1) * TPC)
                pool.wait_ge(S["norm_done"], (k + 1) * TPC)
                g.tensor_tensor(f2_prod[:, mine], xn[:, mine], a2_row[:].unsqueeze(1).broadcast_to([P, TPC, F]), ALU.mult).then_inc(S["f2_prod_done"], 1)

            for k in range(XCH):
                mine = slice(k * TPC, (k + 1) * TPC)
                pool.wait_ge(S["stats_done"], k + 1)
                link(g.tensor_scalar(rstd[:, mine], mv[:, mine, 1], EPS, None, ALU.add))
                g.tensor_tensor(rstd[:, mine], rstd[:, mine], consts[:, 0, mine], ALU.pow).then_inc(S["rstd_done"], 1)
                if k == 0:
                    pool.wait_ge(S["small_in"], 16 * 3)
                if k >= 2:
                    f2_product(k - 2)
            f2_product(XCH - 2)
            f2_product(XCH - 1)
            pool.wait_ge(S["coef_done"], 1)
            link(g.tensor_scalar(coef[:, 0:5], grow[:, 0:5], 1.0, None, ALU.add))
            link(g.tensor_tensor(coef[:, 0:5], coef[:, 0:5], consts[:, 1, 0:5], ALU.pow))
            link(g.tensor_scalar(coef[:, 5:6], coef[:, 2:3], -1.0, 1.0, ALU.mult, ALU.add))
            link(g.tensor_scalar(coef[:, 6:7], coef[:, 1:2], -1.0, 1.0, ALU.mult, ALU.add))
            link(g.tensor_scalar(coef[:, 7:8], coef[:, 0:1], -1.0, 1.0, ALU.mult, ALU.add))
            link(g.tensor_tensor(coef[:, 8:9], coef[:, 6:7], coef[:, 0:1], ALU.mult))
            link(g.tensor_tensor(coef[:, 9:10], coef[:, 6:7], coef[:, 7:8], ALU.mult))
            g.tensor_scalar(coef[:, 10:11], coef[:, 3:4], -1.0, None, ALU.mult).then_inc(S["coef_done"], 1)
            pool.wait_ge(S["fmax_done"], 1)
            g.partition_all_reduce(grow[:, 6:7], grow[:, 5:6], P, bass.bass_isa.ReduceOp.max).then_inc(S["shift_done"], 1)
            end_chain()

            def y_product(q, side, first, prod, done):
                if first:
                    pool.wait_ge(S["colw_done"], 2)
                else:
                    pool.wait_ge(S["mm_done"], R1 - NB + q + 1)
                    pool.wait_ge(S["feat_done"], (q + 1) * JB)
                if q >= 1:
                    pool.wait_ge(S[done], 2 * q - 1 + side)
                w = y_buffer(side)
                if first:
                    g.tensor_copy(w[:, :, F:XC], colw[:, side, q * JB:(q + 1) * JB, :])
                g.tensor_tensor(w[:, :, 0:F], xn[:, q * JB:(q + 1) * JB, :],
                                colw[:, side, q * JB:(q + 1) * JB, 0:1].broadcast_to([P, JB, F]), ALU.mult).then_inc(S[prod], 1)

            for q in range(NB):
                for side in range(2):
                    y_product(q, side, True, "y_prod", "y_done")

            def features(T, k):
                row = g.snap(T) if not isinstance(T, int) else T
                n = {q: small[:, i:i + 1] for i, q in enumerate("E e r zn rho q qz rr s".split())}
                wait(pool, "summed", T + 1)
                pool.wait_ge(S["roww_done"], 2)
                link(g.tensor_copy(small[:, 0:2], roww[:, bass.ds(row, 1), :].rearrange("p a b -> p (a b)")))
                link(g.tensor_tensor(small[:, 12:14], acc_s[:, k, :, F + 1], small[:, 0:1].broadcast_to([P, 2]), ALU.mult))
                link(g.tensor_tensor(num[:], ps_sum[:, k, 0], ps_sum[:, k, 1], ALU.add))
                link(g.tensor_tensor(small[:, 14:16], small[:, 12:14], q_c[:, k], ALU.add))
                link(g.tensor_tensor(n["q"], small[:, 14:15], small[:, 15:16], ALU.add))
                link(g.tensor_scalar(n["zn"], num[:, F:F + 1], 0.0, float(N), ALU.is_equal, ALU.mult))
                link(g.tensor_tensor(n["s"], num[:, F:F + 1], n["zn"], ALU.add))
                link(g.tensor_tensor(n["r"], n["s"], consts[:, 1, 0:1], ALU.pow))
                link(g.tensor_tensor(n["qz"], n["q"], n["zn"], ALU.add))
                link(g.tensor_tensor(n["rr"], n["r"], n["r"], ALU.mult))
                link(g.tensor_tensor(n["rho"], n["qz"], n["rr"], ALU.mult))
                link(g.tensor_scalar(n["rho"], n["rho"], 0.5, None, ALU.mult))
                wait(pool, "feat_done", T - 1)
                if not isinstance(T, int) or T >= 2:
                    feature_sum(T - 2)
                link(g.tensor_tensor(k_one[:, k], coef[:, 5:6], n["rho"], ALU.subtract))
                link(g.tensor_tensor(featw[:, 0], col_mean[:], n["zn"].broadcast_to([P, F]), ALU.mult))
                link(g.tensor_tensor(featw[:, 1], featw[:, 0], num[:, 0:F], ALU.add))
                link(g.tensor_tensor(scaled[:, k], featw[:, 1], n["r"].broadcast_to([P, F]), ALU.mult))
                link(g.tensor_copy(row_out[:, bass.ds(row, 1), :].rearrange("p a b -> p (a b)"), small[:, 2:6]))
                end_chain()
                g.sem_inc(S["scaled_done"], 1)

            def feature_sum(T):
                row = g.snap(T) if not isinstance(T, int) else T
                link(g.tensor_tensor(featsum[:], featsum[:], xn[:, bass.ds(row, 1), :].rearrange("p a b -> p (a b)"), ALU.add))

            link(g.memset(featsum[:], 0.0))
            pool.wait_ge(S["colmean_done"], 1)
            features(0, 0)
            features(1, 1)
            with g.Fori(1, NT // 2 - 1) as u:
                for k in range(2):
                    features(u * 2 + k, k)
            y_product(0, 1, False, "y2_prod_pool", "y2_done")
            features(NT - 2, 0)
            features(NT - 1, 1)
            pool.wait_ge(S["feat_done"], NT)
            feature_sum(NT - 2)
            feature_sum(NT - 1)
            g.sem_inc(S["featsum_done"], 1)

            pool.wait_ge(S["coded"], NG * NT)
            pool.wait_ge(S["signed"], NG * BLOCKS)
            g.affine_select(out=upto, in_=ones[:], compare_op=ALU.is_ge, fill=0.0, base=0, pattern=[[1, P]], channel_multiplier=-1)
            g.affine_select(out=after, in_=ones[:], compare_op=ALU.is_gt, fill=0.0, base=0, pattern=[[-1, P]], channel_multiplier=1)
            pool.wait_ge(S["spilled"], NG * 16)
            pool.wait_ge(S["maskA_ready"], R1)
            pool.wait_ge(S["maskC_ready"], R1)
            g.memset(state[0:DS, 0], 0.0)
            g.memset(hist[:, 0, :, 0:TAPS - 1], 0.0).then_inc(S["halo_done"], 1)

            def base_of(s_, k):
                row = g.snap(s_) if not isinstance(s_, int) else s_
                kap, w, wz = small[:, 12:13], small[:, 14 + k % 2:15 + k % 2], small[:, 13:14]
                wait(pool, f"rowx_in{k % 2}", (s_ - k % 2) * 16 + 32)
                link(g.tensor_copy(small[:, 8:12], row_out[:, bass.ds(row, 1), :].rearrange("p a b -> p (a b)")))
                r, zn, rho = (small[:, i:i + 1] for i in (8, 9, 10))
                link(g.tensor_tensor(kap, coef[:, 1:2], rho, ALU.mult))
                link(g.tensor_tensor(kap, kap, coef[:, 8:9], ALU.add))
                link(g.tensor_tensor(wz, kap, coef[:, 10:11], ALU.mult))
                link(g.tensor_tensor(wz, wz, coef[:, 1:2], ALU.add))
                wait(pool, "x1_done", s_ - 1)
                link(g.tensor_tensor(w, wz, r, ALU.mult))
                link(g.tensor_tensor(wz, w, zn, ALU.mult))
                link(g.tensor_tensor(featw[:, 0], xn[:, bass.ds(row, 1), :].rearrange("p a b -> p (a b)"),
                                     kap.broadcast_to([P, F]), ALU.mult))
                link(g.tensor_tensor(featw[:, 1], h0_in[:, k % 2], coef[:, 9:10].broadcast_to([P, F]), ALU.mult))
                link(g.tensor_tensor(featw[:, 0], featw[:, 0], featw[:, 1], ALU.add))
                link(g.tensor_tensor(featw[:, 0], featw[:, 0], x_in[:, k % 2], ALU.add))
                pool.wait_ge(S["colmean_done"], 2)
                link(g.tensor_tensor(featw[:, 1], col_mean[:], wz.broadcast_to([P, F]), ALU.mult))
                link(g.tensor_tensor(base[:, k % 2], featw[:, 0], featw[:, 1], ALU.add))
                g.sem_inc(S["base_done"], 1)

            def heads(ap, width):
                return ap.rearrange("p (h w) -> p h w", h=NH)

            def slot(s_, k, now, then, ok):
                if ok[0]:
                    kt = (k - 1) % SLOTS
                    wait(pool, "ln_done", s_)
                    wait(pool, "xn2_ready", s_ - 1)
                    link(g.tensor_tensor(tiny[:, 1, 0:1], tiny[:, 0, 1:2], consts[:, 2, 0:1], ALU.add))
                    g.tensor_tensor(tiny[:, 1, 1:2], tiny[:, 1, 0:1], consts[:, 0, 0:1], ALU.pow).then_inc(S["rstd2"], 1)
                    wait(pool, "out_done", s_ - 4)
                    g.tensor_tensor(x1b[:, kt], x1[:, kt % 2], b_row, ALU.add).then_inc(S["x1b_done"], 1)
                if now:
                    base_of(s_, k)
                if ok[1]:
                    wait(pool, "dt_ready", s_ - 1)
                    wait(pool, "p_cum", s_ - 2)
                    g.tensor_tensor(dam, upto.unsqueeze(1).broadcast_to([P, NH, P]),
                                    tiny[:, 2 + k % 2, NH:2 * NH].unsqueeze(2).broadcast_to([P, NH, P]), ALU.mult).then_inc(S["dam_ready"], 1)
                if ok[2]:
                    kc = (k - 3) % 2
                    wait(pool, "xl_ready", s_ - 2)
                    wait(pool, "p_y", s_ - 3)
                    dtc = tiny[:, 2 + kc, 0:NH]
                    link(g.tensor_tensor(heads(xdt, HD), heads(xl[:, 0:DI], HD), dtc.unsqueeze(2).broadcast_to([P, NH, HD]), ALU.mult))
                    wait(pool, "exp_done", s_ - 2)
                    g.tensor_tensor(heads(xdtd, HD), heads(xdt, HD), expD[:, :, P - 1:P].broadcast_to([P, NH, HD]), ALU.mult).then_inc(S["xdt_ready"], 1)
                    wait(pool, "y_read", s_ - 3)
                    g.tensor_tensor(heads(xD, HD), heads(xl[:, 0:DI], HD), d_row.unsqueeze(2).broadcast_to([P, NH, HD]), ALU.mult).then_inc(S["xD_ready"], 1)
                    wait(pool, "st_done", s_ - 3)
                    g.tensor_tensor(heads(pstate[0:DS], HD), heads(state[0:DS, kc], HD),
                                    tiny[0:DS, 4 + kc, NH:2 * NH].unsqueeze(2).broadcast_to([DS, NH, HD]), ALU.mult).then_inc(S["ps_ready"], 1)
                if ok[3]:
                    wait(pool, "ssq_ready", s_ - 3)
                    wait(pool, "out_done", s_ - 4)
                    link(g.tensor_tensor(tiny[:, 6, 0:1], tiny[:, 6, 1:2], consts[:, 3, 0:1], ALU.add))
                    g.tensor_tensor(tiny[:, 6, 2:3], tiny[:, 6, 0:1], consts[:, 0, 0:1], ALU.pow).then_inc(S["rs_ready"], 1)
                end_chain()

            pool.wait_ge(S["w_in"], 16 * 12)
            schedule(g, slot)

        @block.vector
        def _(dve):
            v = nc.vector
            def statistics(k):
                dve.wait_ge(S[f"x_in{k}"], 16)
                for t in range(k * TPC, (k + 1) * TPC):
                    v.bn_stats(stats[:, t, :], xn[:, t, :]).then_inc(S["vch"], 1)
                for t in range(k * TPC, (k + 1) * TPC):
                    dve.wait_ge(S["vch"], t + 1)
                    last = v.bn_aggr(mv[:, t, :], stats[:, t, :])
                last.then_inc(S["stats_done"], 1)

            def normalise(k):
                dve.wait_ge(S["rstd_done"], k + 1)
                for t in range(k * TPC, (k + 1) * TPC):
                    v.tensor_scalar(xn[:, t, :], xn[:, t, :], mv[:, t, 0:1], rstd[:, t:t + 1], ALU.subtract, ALU.mult).then_inc(S["norm_done"], 1)

            statistics(0)
            dve.wait_ge(S["small_in"], 16 * 3)
            dve.wait_ge(S["const_ready"], 1)
            v.tensor_scalar(a1_wide[:], ones[:], a_col[:, 0:1], None, ALU.mult).then_inc(S["a1_ready"], 1)
            for k in range(1, XCH):
                statistics(k)
                normalise(k - 1)
            normalise(XCH - 1)
            for k in range(XCH):
                mine = slice(k * TPC, (k + 1) * TPC)
                dve.wait_ge(S["f2_prod_done"], k + 1)
                v.tensor_reduce(fcol[:, mine, 1], f2_prod[:, mine], AX_X, ALU.add).then_inc(S["f2_copied"], 1)
            dve.wait_ge(S["f2_copied"], XCH)
            v.tensor_reduce(grow[:, 5:6], fcol[:, :, 1], AX_X, ALU.max).then_inc(S["fmax_done"], 1)
            v.tensor_scalar(neg_f2[:], fcol[:, :, 1], -1.0, None, ALU.mult).then_inc(S["f2_copied"], 1)
            dve.wait_ge(S["shift_done"], 1)
            v.tensor_scalar(grow[:, 7:8], grow[:, 6:7], -1.0, SHIFT, ALU.mult, ALU.add)
            v.tensor_scalar(grow[:, 5:6], grow[:, 6:7], -SLOPE, None, ALU.mult).then_inc(S["bias_ready"], 1)
            dve.wait_ge(S["f2_copied"], XCH + 1)
            dve.wait_ge(S["colw_done"], 1)
            v.tensor_tensor(colw[:, :, :, 1], colw[:, :, :, 0], colw[:, :, :, 0], ALU.mult).then_inc(S["colw_done"], 1)
            def y_product(q, side, prod, done):
                dve.wait_ge(S["mm_done"], R1 - NB + q + 1)
                dve.wait_ge(S["feat_done"], (q + 1) * JB)
                if q >= 1:
                    dve.wait_ge(S[done], 2 * q - 1 + side)
                v.tensor_tensor(y_buffer(side)[:, :, 0:F], xn[:, q * JB:(q + 1) * JB, :],
                                colw[:, side, q * JB:(q + 1) * JB, 0:1].broadcast_to([P, JB, F]), ALU.mult).then_inc(S[prod], 1)

            def y_low(q, side, cols, hi, done):
                dve.wait_ge(S[hi], 2 * q + side + 1)
                v.tensor_tensor(Y[:, q * JB:(q + 1) * JB, side, 1, 0:cols], y_buffer(side)[:, :, 0:cols],
                                Y[:, q * JB:(q + 1) * JB, side, 0, 0:cols].bitcast(F32), ALU.subtract).then_inc(S[done], 1)

            def y_second(q):
                y_product(q, 0, "y2_prod", "y2_done")
                if q > 0:
                    y_product(q, 1, "y2_prod", "y2_done")
                y_low(q, 0, F, "y2_hi", "y2_done")
                y_low(q, 1, F, "y2_hi", "y2_done")

            def codes(G, par, jt):
                n = G * NT + jt
                dve.wait_ge(S["tr_done"], n + 1)
                rows = bass.ds(v.snap(G * 512) if not isinstance(G, int) else G * 512, 512)
                v.scalar_tensor_tensor(
                    out=code[:, par, :, jt * P:(jt + 1) * P], in0=f1_rows[:, rows].rearrange("p (i r) -> p i r", i=IT),
                    scalar=neg_f2[:, jt:jt + 1], in1=ps[jt % TRB][:, :].rearrange("p (i r) -> p i r", i=IT),
                    op0=ALU.is_gt, op1=ALU.add).then_inc(S["coded"], 1)

            def mask_c(n, src, b):
                wait(dve, "mm_done", n - (MASKS - 1))
                v.tensor_scalar(maskC[:, b % MASKS], src, 2.0, None, ALU.is_equal).then_inc(S["maskC_ready"], 1)

            def mask1(G, par, b):
                if b >= BLOCKS:
                    G, par, b = G + 1, 1 - par, b - BLOCKS
                it, ch = b // NB, b % NB
                dve.wait_ge(S["coded"], G * NT + (NT if it else (ch + 1) * JB))
                mask_c(G * BLOCKS + b, code[:, par, it, ch * JB * P:(ch + 1) * JB * P], b)

            def sum1(T, k):
                row = v.snap(T) if not isinstance(T, int) else T
                w = roww[:, bass.ds(row, 1), 1:2].rearrange("p a b -> p (a b)")
                dve.wait_ge(S["acc_read"], T + 1)
                wait(dve, "scaled_done", T - 1)
                both = accC[k][:, 0:2 * XC].rearrange("p (a b) -> p a b", a=2)
                v.tensor_scalar(q_c[:, k], both[:, :, F + 1], w, w, ALU.mult, ALU.mult)
                v.scalar_tensor_tensor(out=ps_sum[:, k], in0=both, scalar=w, in1=acc_s[:, k], op0=ALU.mult, op1=ALU.add).then_inc(S["summed"], 1)

            def feat1(T, k):
                row = v.snap(T) if not isinstance(T, int) else T
                mine = xn[:, bass.ds(row, 1), :].rearrange("p a b -> p (a b)")
                wait(dve, "feat_done", T)
                dve.wait_ge(S["scaled_done"], T + 1)
                link(v.scalar_tensor_tensor(out=fwork[:, 0], in0=mine, scalar=k_one[:, k], in1=scaled[:, k], op0=ALU.mult, op1=ALU.add))
                link(v.tensor_scalar(fwork[:, 1], fwork[:, 0], -THRESH, THRESH, ALU.max, ALU.min))
                v.tensor_tensor(mine, fwork[:, 0], fwork[:, 1], ALU.subtract).then_inc(S["feat_done"], 1)
                end_chain()

            def supertile(G, par, first=False, last=False):
                for b in range(BLOCKS):
                    it, ch = b // NB, b % NB
                    if not (last and b + LEAD >= BLOCKS):
                        mask1(G, par, b + LEAD)
                    if not last:
                        if b == 0:
                            wait(dve, "maskA_ready", G * BLOCKS)
                            wait(dve, "spilled", G * 16)
                        for j in range(JH):
                            codes(G + 1, 1 - par, b * JH + j)
                    if ch == 2 and not (first and it < 1):
                        sum1(G * IT + (it - 1), (it - 1) % 2)
                    if ch == 2 and not (first and it < 2):
                        feat1(G * IT + (it - 2), it % 2)

            chain = [0]

            def step(ins):
                chain[0] += 1
                ins.then_inc(S["vch"], 1)
                return chain[0]

            def link(ins):
                dve.wait_ge(S["vch"], step(ins))

            def end_chain():
                if chain[0]:
                    dve.wait_ge(S["vch"], chain[0])
                    v.sem_clear(S["vch"])
                chain[0] = 0

            chain[0] = NT
            end_chain()
            for q in range(NB):
                for jt in range(q * JB, (q + 1) * JB):
                    codes(0, 0, jt)
                y_low(q, 0, XC, "y_hi", "y_done")
                y_low(q, 1, XC, "y_hi", "y_done")
                if q < LEAD:
                    mask1(0, 0, q)
                if q == 0:
                    dve.wait_ge(S["fcol_done"], 1)
                    v.tensor_copy(fcol[:, :, 0], accA[1][:, 0:NT]).then_inc(S["fcol_copied"], 1)
                    dve.wait_ge(S["fcol_copied"], 1)
                    step(v.tensor_scalar(hcol[:, 0], fcol[:, :, 0], grow[:, 6:7], 1.0 - SLOPE, ALU.add, ALU.mult))
                    link(v.tensor_scalar(hcol[:, 1], fcol[:, :, 0], grow[:, 6:7], SLOPE - 1.0, ALU.add, ALU.mult))
                    v.tensor_scalar(hcol[:, 0], hcol[:, 0], 0.0, -SHIFT, ALU.min, ALU.add)
                    v.tensor_scalar(hcol[:, 1], hcol[:, 1], 0.0, None, ALU.min).then_inc(S["roww_done"], 1)
                    end_chain()
            dve.wait_ge(S["sums_done"], 1)
            v.tensor_scalar(col_mean[:], accC[1][:, 0:F], 1.0 / N, None, ALU.mult).then_inc(S["colmean_done"], 1)
            supertile(0, 0, first=True)
            with v.Fori(0, NG // 2 - 1) as u:
                supertile(u * 2 + 1, 1)
                supertile(u * 2 + 2, 0)
            supertile(NG - 1, 1, last=True)

            def mask2(n, k, j):
                b = j % NB
                dve.wait_ge(S[f"codes_in{k}"], code_count(n, k, b))
                mask_c(n + R1, code[:, 0, k, b * JB * P:(b + 1) * JB * P], b)

            y_second(0)
            mask2(0, 0, 0)
            sum1(NT - 1, 1)
            y_second(1)
            mask2(1, 0, 1)
            feat1(NT - 2, 0)
            dve.wait_ge(S["w_in"], 16 * 12)
            v.tensor_scalar(w_zdt[:, 0:DI], w_zdt[:, 0:DI], 0.5, None, ALU.mult)
            v.tensor_scalar(conv_wt, conv_wt, 0.5, None, ALU.mult)
            v.tensor_scalar(conv_bt, conv_bt, 0.5, None, ALU.mult).then_inc(S["w_ready"], 1)
            y_second(2)
            mask2(2, 0, 2)
            mask2(3, 0, 3)
            feat1(NT - 1, 1)
            dve.wait_ge(S["w_turned"], 1)
            v.tensor_copy(w_outT, ps[1][:, 0:KB * P].rearrange("p (k n) -> p k n", k=KB)).then_inc(S["w_copied"], 1)
            y_second(3)
            dve.wait_ge(S["w_ready"], 2)
            v.tensor_scalar(a_row, a_row, -1.0, None, ALU.mult).then_inc(S["w_done"], 1)

            def series(z):
                root = np.sqrt(z)
                return np.where(z > 1e-8, 2 * np.arctanh(root) / np.maximum(root, 1e-9), 2 + 2 * z / 3)

            top = 1.0 / 9.0
            points = top / 2 * (1 - np.cos(np.pi * (np.arange(64) + 0.5) / 64))
            log_c = [float(c) for c in np.polynomial.Polynomial.fit(points, series(points), 5, domain=[0, top]).convert().coef]

            def heads(ap):
                return ap.rearrange("p (h w) -> p h w", h=NH)

            def slot(s_, k, now, then, ok):
                def mask(j):
                    if (now and not (isinstance(s_, int) and s_ == 0) if j + LEAD < NB else then):
                        mask2(s_ * NB + (j + LEAD), (k + (j + LEAD) // NB) % SLOTS, j + LEAD)

                k2 = k % 2
                kt = (k - 1) % 2
                part = sum2.rearrange("p (a b) -> p a b", a=2)
                if ok[4]:
                    dve.wait_ge(S["p_o"], s_ - 4)
                if ok[3]:
                    dve.wait_ge(S["p_g"], s_ - 3)
                    masked = step(v.tensor_tensor(gm, ps[1][:, 0:P], upto, ALU.mult))
                if ok[0]:
                    T = s_ - 1
                    row = v.snap(T) if not isinstance(T, int) else T
                    dve.wait_ge(S["acc_read"], T + (NT + 1))
                    dve.wait_ge(S["base_done"], T + 1)
                    halves = step(v.scalar_tensor_tensor(
                        out=part, in0=accC[kt][:, 0:2 * F].rearrange("p (a b) -> p a b", a=2),
                        scalar=roww[:, bass.ds(row, 1), 1:2].rearrange("p a b -> p (a b)"), in1=acc_s[:, kt, :, 0:F], op0=ALU.mult, op1=ALU.add))
                if ok[3]:
                    dve.wait_ge(S["vch"], masked)
                    dve.wait_ge(S["exp_done"], s_ - 3)
                    wait(dve, "p_y", s_ - 4)
                    v.tensor_tensor(wmix, expD, gm.unsqueeze(1).broadcast_to([P, NH, P]), ALU.mult).then_inc(S["mix_ready"], 1)
                mask(0)
                if ok[4]:
                    dve.wait_ge(S["rs_ready"], s_ - 4)
                    wait(dve, f"stored{1 - k2}", (s_ - 5 - (1 - k2)) * 8)
                    v.scalar_tensor_tensor(out=outb[:, 1 - k2], in0=ps[1][:, P:P + F], scalar=tiny[:, 6, 2:3], in1=x1b[:, (k - 1) % SLOTS],
                                           op0=ALU.mult, op1=ALU.add).then_inc(S["out_done"], 1)
                if ok[0]:
                    dve.wait_ge(S["vch"], halves)
                    halves = step(v.tensor_tensor(part[:, 0], part[:, 0], part[:, 1], ALU.add))
                if ok[0]:
                    dve.wait_ge(S["vch"], halves)
                    wait(dve, "x1b_done", T - 1)
                    v.scalar_tensor_tensor(out=x1[:, kt], in0=part[:, 0], scalar=small[:, 14 + kt:15 + kt], in1=base[:, kt],
                                           op0=ALU.mult, op1=ALU.add).then_inc(S["x1_done"], 1)
                mask(1)
                if isinstance(s_, int) and s_ == 0:
                    dve.wait_ge(S["w_mult"], 1)
                    for kb in range(KB):
                        v.tensor_scalar(w_comb[:, kb], ps[2][:, kb * P:(kb + 1) * P], normw[:, kb:kb + 1], float(np.sqrt(DI)), ALU.mult, ALU.mult)
                    dve.wait_ge(S["ysum_done"], 1)
                    v.tensor_scalar(col_mean[:], ps[3][:, 0:F], 1.0 / N, None, ALU.mult).then_inc(S["colmean_done"], 1)
                if ok[0]:
                    dve.wait_ge(S["x1_done"], T + 1)
                    seen = step(v.bn_stats(tiny[:, 7, 0:6], x1[:, kt]))
                if ok[1]:
                    dve.wait_ge(S["in_read"], s_ - 1)
                    wait(dve, "ew_ready", s_ - 2)
                    logit = step(v.tensor_tensor(tiny[:, 8, 0:NH], zdt[:, DI:DI + NH], dt_b, ALU.add))
                    dve.wait_ge(S["halo_done"], s_ - 1)
                    taps = [(tap, cb) for tap in range(TAPS - 1) for cb in range(CB)]
                    made = {}

                    def conv_step(i):
                        tap, cb = taps[i]
                        if tap:
                            dve.wait_ge(S["vch"], made[cb])
                        ins = v.scalar_tensor_tensor(out=conv[:, cb], in0=hist[:, k2, cb, tap:tap + P], scalar=conv_wt[:, cb, tap:tap + 1],
                                                     in1=conv[:, cb], op0=ALU.mult, op1=ALU.add)
                        if i == len(taps) - 1:
                            ins.then_inc(S["conv_pre"], 1)
                        else:
                            made[cb] = step(ins)

                    conv_step(0)
                if ok[0]:
                    dve.wait_ge(S["vch"], seen)
                    v.bn_aggr(tiny[:, 0, 0:2], tiny[:, 7, 0:6]).then_inc(S["ln_done"], 1)

                def normalise2():
                    if ok[0]:
                        dve.wait_ge(S["rstd2"], s_)
                        wait(dve, "p_xT", s_ - 2)
                        v.tensor_scalar(xn2[:, kt], x1[:, kt], tiny[:, 0, 0:1], tiny[:, 1, 1:2], ALU.subtract, ALU.mult).then_inc(S["xn2_ready"], 1)

                summed_y = [0]

                def y_state():
                    if ok[3]:
                        dve.wait_ge(S["p_y"], s_ - 3)
                        dve.wait_ge(S["xD_ready"], s_ - 3)
                        dve.wait_ge(S["ps_ready"], s_ - 3)
                        summed_y[0] = step(v.tensor_tensor(heads(ysum), heads(ps[0][:, DI:2 * DI]),
                                                           tiny[:, 4 + k2, 0:NH].unsqueeze(2).broadcast_to([P, NH, HD]), ALU.mult))
                        v.tensor_tensor(state[0:DS, 1 - k2], pstate[0:DS], ps[1][0:DS, 0:DI], ALU.add).then_inc(S["st_done"], 1)

                def y_skip():
                    if ok[3]:
                        dve.wait_ge(S["vch"], summed_y[0])
                        summed_y[0] = step(v.tensor_tensor(ysum, ysum, xD, ALU.add))

                def y_within():
                    if ok[3]:
                        dve.wait_ge(S["vch"], summed_y[0])
                        v.tensor_tensor(ysum, ysum, ps[0][:, 0:DI], ALU.add).then_inc(S["y_read"], 1)

                if ok[1]:
                    dve.wait_ge(S["vch"], logit)
                    v.scalar_tensor_tensor(out=tiny[:, 9, 0:NH], in0=tiny[:, 8, 0:NH], scalar=-1.0, in1=tiny[:, 8, 0:NH],
                                           op0=ALU.mult, op1=ALU.min).then_inc(S["nv_ready"], 1)
                    e, two, si, z, p = (tiny[:, i, 0:NH] for i in (10, 11, 12, 13, 14))
                    for i in range(1, 4):
                        conv_step(i)
                    dve.wait_ge(S["ew_ready"], s_ - 1)
                    last = step(v.tensor_scalar(two, e, 2.0, None, ALU.add))
                    conv_step(4)
                    dve.wait_ge(S["vch"], last)
                    last = step(v.reciprocal(two, two))
                    conv_step(5)
                    dve.wait_ge(S["vch"], last)
                    last = step(v.tensor_tensor(si, e, two, ALU.mult))
                    conv_step(6)
                    dve.wait_ge(S["vch"], last)
                    last = step(v.tensor_tensor(z, si, si, ALU.mult))
                    conv_step(7)
                    dve.wait_ge(S["vch"], last)
                    last = step(v.tensor_scalar(p, z, log_c[-1], None, ALU.mult))
                    conv_step(8)
                    others = [None, None, normalise2, y_state, y_skip]
                    for cf, other in zip(log_c[-2:0:-1] + [None], others):
                        dve.wait_ge(S["vch"], last)
                        if cf is None:
                            last = step(v.scalar_tensor_tensor(out=p, in0=p, scalar=log_c[0], in1=si, op0=ALU.add, op1=ALU.mult))
                        else:
                            last = step(v.scalar_tensor_tensor(out=p, in0=p, scalar=cf, in1=z, op0=ALU.add, op1=ALU.mult))
                        if other is not None:
                            other()
                    wait(dve, "xdt_ready", s_ - 3)
                    wait(dve, "p_cum", s_ - 3)
                    dve.wait_ge(S["vch"], last)
                    last = step(v.scalar_tensor_tensor(out=tiny[:, 2 + k2, 0:NH], in0=tiny[:, 8, 0:NH], scalar=0.0, in1=p, op0=ALU.max, op1=ALU.add))
                    y_within()
                    dve.wait_ge(S["vch"], last)
                    v.tensor_tensor(tiny[:, 2 + k2, NH:2 * NH], tiny[:, 2 + k2, 0:NH], a_row, ALU.mult).then_inc(S["dt_ready"], 1)
                else:
                    normalise2()
                    y_state()
                    y_skip()
                    y_within()
                if ok[3]:
                    dve.wait_ge(S["y_read"], s_ - 3)
                    wait(dve, "p_yT", s_ - 4)
                    wait(dve, "ssq_ready", s_ - 4)
                    v.tensor_tensor(yg, ysum, gate[:, k2], ALU.mult).then_inc(S["yg_ready"], 1)
                mask(2)
                if ok[1]:
                    dve.wait_ge(S["zt_ready"], s_ - 1)
                    wait(dve, "yg_ready", s_ - 3)
                    v.scalar_tensor_tensor(out=gate[:, k2], in0=ztan, scalar=1.0, in1=zdt[:, 0:DI], op0=ALU.add, op1=ALU.mult).then_inc(S["gate_done"], 1)
                    dve.wait_ge(S["ctan_ready"], s_ - 1)
                    v.scalar_tensor_tensor(out=xbc[:, k2], in0=gate_t, scalar=1.0, in1=conv, op0=ALU.add, op1=ALU.mult).then_inc(S["conv_ready"], 1)
                mask(3)
                end_chain()

            schedule(v, slot)

        @block.scalar
        def _(act):
            s = nc.scalar
            s.preload_act_table_set("exp_and_others")
            act.wait_ge(S["small_in"], 16 * 3)
            s.activation(grow[:, 0:5], grow[:, 0:5], ACT.Exp, scale=-1.0).then_inc(S["coef_done"], 1)
            for q in range(NT // 4 + 1):
                if q < NT // 4:
                    act.wait_ge(S["xT_done"], q + 1)
                    s.copy(xnT[:, q * 512:(q + 1) * 512], accA[q % 2][:, :]).then_inc(S["xT_copied"], 1)
                if q >= 1:
                    act.wait_ge(S["f1_done"], q)
                    s.copy(f1_rows[:, (q - 1) * 512:q * 512], ps[1 + (q - 1) % 2][:, :]).then_inc(S["f1_copied"], 1)
            act.wait_ge(S["bias_ready"], 1)
            s.activation(colw[:, 0, :, 0], fcol[:, :, 1], ACT.Exp, bias=grow[:, 7:8])
            s.activation(colw[:, 1, :, 0], fcol[:, :, 1], ACT.Exp, bias=grow[:, 5:6], scale=SLOPE).then_inc(S["colw_done"], 1)

            def y_high(q, cols, prods, hi):
                for side in range(2):
                    name, count = prods[side]
                    act.wait_ge(S[name], count)
                    s.copy(Y[:, q * JB:(q + 1) * JB, side, 0, 0:cols], y_buffer(side)[:, :, 0:cols]).then_inc(S[hi], 1)

            def sign(G, h, first=False):
                n = G * BLOCKS + h
                act.wait_ge(S[f"adj_in{h % 4}"], (G * 4 + (h // 4 + 1)) * 16)
                if not first:
                    act.wait_ge(S["tr_done"], n * 2 - 6)
                s.activation(edges[:, h % 4], adj_in[:, h % 4], ACT.Sign).then_inc(S["signed"], 1)

            def mask_a(n, src, b):
                wait(act, "mm_done", n - (MASKS - 1))
                s.activation(maskA[:, b % MASKS], src, ACT.Relu, bias=-2.0).then_inc(S["maskA_ready"], 1)

            def mask1(G, par, b):
                if b >= BLOCKS:
                    G, par, b = G + 1, 1 - par, b - BLOCKS
                it, ch = b // NB, b % NB
                act.wait_ge(S["coded"], G * NT + (NT if it else (ch + 1) * JB))
                mask_a(G * BLOCKS + b, code[:, par, it, ch * JB * P:(ch + 1) * JB * P], b)

            def read_acc(T, k, cols, round_two=0):
                row = s.snap(T) if not isinstance(T, int) else T
                act.wait_ge(S["mm_done"], T * NB + (NB + round_two * R1))
                if round_two:
                    wait(act, "x1_done", T - 1)
                else:
                    wait(act, "scaled_done", T - 1)
                w = roww[:, bass.ds(row, 1), 0:1].rearrange("p a b -> p (a b)")
                src = accA[k][:, 0:2 * cols].rearrange("p (a b) -> p a b", a=2)
                s.mul(acc_s[:, k, :, 0:cols], src, w).then_inc(S["acc_read"], 1)

            def supertile(G, par, first=False, last=False):
                for b in range(BLOCKS):
                    it, ch = b // NB, b % NB
                    if not (last and b + LEAD >= BLOCKS):
                        mask1(G, par, b + LEAD)
                    if not last:
                        sign(G + 1, b)
                    if ch == 1 and not (first and it == 0):
                        read_acc(G * IT + (it - 1), (it - 1) % 2, XC)

            for q in range(NB):
                for h in range(q * 4, q * 4 + 4):
                    sign(0, h, first=h < 4)
                y_high(q, XC, (("y_prod", 2 * q + 1), ("y_prod", 2 * q + 2)), "y_hi")
                if q >= 1 and q - 1 < LEAD:
                    mask1(0, 0, q - 1)
                if q == 1:
                    act.wait_ge(S["roww_done"], 1)
                    s.activation(roww[:, :, 0], hcol[:, 0], ACT.Exp)
                    s.activation(roww[:, :, 1], hcol[:, 1], ACT.Exp).then_inc(S["roww_done"], 1)
            supertile(0, 0, first=True)
            with s.Fori(0, NG // 2 - 1) as u:
                supertile(u * 2 + 1, 1)
                supertile(u * 2 + 2, 0)
            supertile(NG - 1, 1, last=True)

            def mask2(n, k, j):
                b = j % NB
                act.wait_ge(S[f"codes_in{k}"], code_count(n, k, b))
                mask_a(n + R1, code[:, 0, k, b * JB * P:(b + 1) * JB * P], b)

            y_high(0, F, (("y2_prod", 1), ("y2_prod_pool", 1)), "y2_hi")
            mask2(0, 0, 0)
            read_acc(NT - 1, 1, XC)
            y_high(1, F, (("y2_prod", 2), ("y2_prod", 3)), "y2_hi")
            mask2(1, 0, 1)
            act.wait_ge(S["w_in"], 16 * 12)
            s.activation(a_row, a_row, ACT.Exp).then_inc(S["w_ready"], 1)
            y_high(2, F, (("y2_prod", 4), ("y2_prod", 5)), "y2_hi")
            mask2(2, 0, 2)
            mask2(3, 0, 3)
            y_high(3, F, (("y2_prod", 6), ("y2_prod", 7)), "y2_hi")

            def slot(s_, k, now, then, ok):
                def mask(j):
                    if (now and not (isinstance(s_, int) and s_ == 0) if j + LEAD < NB else then):
                        mask2(s_ * NB + (j + LEAD), (k + (j + LEAD) // NB) % SLOTS, j + LEAD)

                if ok[0]:
                    read_acc(s_ - 1, (k - 1) % 2, F, 1)
                if ok[1]:
                    act.wait_ge(S["p_xT"], s_ - 1)
                    wait(act, "p_in", s_ - 2)
                    s.copy(xn2T, ps[0][:, 0:P]).then_inc(S["xT_ready"], 1)
                mask(0)
                if ok[1]:
                    kc = k % 2
                    act.wait_ge(S["p_in"], s_ - 1)
                    wait(act, "dt_ready", s_ - 2)
                    wait(act, "gate_done", s_ - 2)
                    s.copy(zdt, ps[2][:, 0:DI + NH]).then_inc(S["zcopy"], 1)
                    wait(act, "conv_pre", s_ - 3)
                    s.copy(hist[:, kc, :, TAPS - 1:], ps[3][:, 0:CB * P].rearrange("p (c w) -> p c w", c=CB))
                    wait(act, "conv_ready", s_ - 2)
                    for cb in range(CB):
                        m = s.activation(conv[:, cb], ps[3][:, cb * P:(cb + 1) * P], ACT.Identity, bias=conv_bt[:, cb:cb + 1],
                                         scale=conv_wt[:, cb, TAPS - 1:TAPS])
                    m.then_inc(S["in_read"], 1)
                    act.wait_ge(S["in_read"], s_ - 1)
                    wait(act, "conv_pre", s_ - 2)
                    s.copy(hist[:, 1 - kc, :, 0:TAPS - 1], hist[:, kc, :, P:P + TAPS - 1]).then_inc(S["halo_done"], 1)
                    act.wait_ge(S["nv_ready"], s_ - 1)
                    wait(act, "dt_ready", s_ - 2)
                    s.activation(tiny[:, 10, 0:NH], tiny[:, 9, 0:NH], ACT.Exp).then_inc(S["ew_ready"], 1)
                mask(1)
                if ok[1]:
                    act.wait_ge(S["zcopy"], s_ - 1)
                    s.activation(ztan, zdt[:, 0:DI], ACT.Tanh).then_inc(S["zt_ready"], 1)
                mask(2)
                if ok[1]:
                    act.wait_ge(S["conv_pre"], s_ - 1)
                    wait(act, "conv_ready", s_ - 2)
                    s.activation(gate_t, conv, ACT.Tanh).then_inc(S["ctan_ready"], 1)
                if ok[2]:
                    kc = (k - 3) % 2
                    act.wait_ge(S["p_cum"], s_ - 2)
                    wait(act, "p_y", s_ - 3)
                    wait(act, "xD_ready", s_ - 3)
                    s.copy(xl, ps[2][:, P:P + CB * P]).then_inc(S["xl_ready"], 1)
                    wait(act, "y_read", s_ - 4)
                    wait(act, "ps_ready", s_ - 4)
                    s.activation(tiny[:, 4 + kc, :], ps[2][:, 0:2 * NH], ACT.Exp)
                    wait(act, "mix_ready", s_ - 3)
                    wait(act, "xdt_ready", s_ - 3)
                    s.activation(expD, ps[3][:, 0:NH * P].rearrange("p (h w) -> p h w", h=NH), ACT.Exp).then_inc(S["exp_done"], 1)
                    act.wait_ge(S["p_ct"], s_ - 2)
                    s.copy(cT[0:DS], ps[1][0:DS, 2 * P:3 * P]).then_inc(S["cT_ready"], 1)
                if ok[3]:
                    act.wait_ge(S["p_yT"], s_ - 3)
                    wait(act, "p_o", s_ - 4)
                    s.copy(yT, ps[3][:, 0:DI].rearrange("p (c w) -> p c w", c=KB)).then_inc(S["yT_ready"], 1)
                    wait(act, "rs_ready", s_ - 4)
                    act.wait_ge(S["yg_ready"], s_ - 3)
                    wait(act, "ssq_ready", s_ - 4)
                    s.activation(junk, yg, ACT.Square, accum_out=tiny[:, 6, 1:2]).then_inc(S["ssq_ready"], 1)
                mask(3)

            schedule(s, slot)

        @block.tensor
        def _(pe):
            t_ = nc.tensor
            pe.wait_ge(S["const_ready"], 1)
            for q in range(NT // 4 + 1):
                if q < NT // 4:
                    if q >= 2:
                        pe.wait_ge(S["xT_copied"], q - 1)
                    for t in range(q * 4, q * 4 + 4):
                        pe.wait_ge(S["norm_done"], t + 1)
                        m = t_.transpose(accA[q % 2][:, (t % 4) * P:(t % 4 + 1) * P], xn[:, t, :], ident[:])
                    m.then_inc(S["xT_done"], 1)
                if q >= 1:
                    if q == 1:
                        pe.wait_ge(S["small_in"], 16 * 3)
                        pe.wait_ge(S["a1_ready"], 1)
                    c = q - 1
                    pe.wait_ge(S["xT_copied"], q)
                    if c >= 2:
                        pe.wait_ge(S["f1_copied"], c - 1)
                    t_.matmul(ps[1 + c % 2][:, :], a1_wide[:], xnT[:, c * 512:(c + 1) * 512], start=True, stop=True).then_inc(S["f1_done"], 1)

            for t in range(NT):
                m = t_.matmul(accA[1][:, t:t + 1], xnT[:, t * P:(t + 1) * P], a_col[:, 0:1], start=True, stop=True)
            m.then_inc(S["fcol_done"], 1)
            pe.wait_ge(S["f1_copied"], 8)

            def turn(G, b, first=False):
                pe.wait_ge(S["signed"], G * BLOCKS + b + 1)
                for j in range(JH):
                    jt = b * JH + j
                    if not (first and jt < TRB):
                        pe.wait_ge(S["coded"], G * NT + (jt - TRB + 1))
                    for it in range(IT):
                        m = t_.matmul(ps[jt % TRB][:, it * P:(it + 1) * P], edges[:, b % 4, it, j * P:(j + 1) * P], ident2[:], start=True, stop=True)
                    m.then_inc(S["tr_done"], 1)

            def products(n, k, b, ch, cols, y=None, between=None):
                pe.wait_ge(S["maskA_ready"], n + 1)
                if y is not None:
                    pe.wait_ge(y, 2 * ch + 2)
                for l in range(JB):
                    jt = ch * JB + l
                    t_.matmul(accA[k][:, 0:2 * cols], maskA[:, b % MASKS, l * P:(l + 1) * P], Y[:, jt, 0, :, 0:cols],
                              start=jt == 0, stop=jt == NT - 1)
                if between is not None:
                    between()
                pe.wait_ge(S["maskC_ready"], n + 1)
                for l in range(JB):
                    jt = ch * JB + l
                    m = t_.matmul(accC[k][:, 0:2 * cols], maskC[:, b % MASKS, l * P:(l + 1) * P], Y[:, jt, 1, :, 0:cols],
                                  start=jt == 0, stop=jt == NT - 1)
                m.then_inc(S["mm_done"], 1)

            def supertile(G, par, first=False, last=False):
                for b in range(BLOCKS):
                    it, ch = b // NB, b % NB
                    if first and b < LEAD:
                        turn(G + 1, b)
                        continue
                    if first and b == NB:
                        pe.wait_ge(S["colmean_done"], 1)
                    if ch == 0 and not (first and it < 2):
                        free_acc(G * IT + (it - 2))
                    products(G * BLOCKS + b, it % 2, b, ch, XC, S["y_done"] if first and it == 0 else None)
                    if not last:
                        turn(G + 1, b)

            def free_acc(T):
                pe.wait_ge(S["acc_read"], T + 1)
                pe.wait_ge(S["summed"], T + 1)

            for q in range(NB):
                for b in range(q * 4, q * 4 + 4):
                    turn(0, b, first=True)
                if q >= 1 and q - 1 < LEAD:
                    products(q - 1, 0, q - 1, q - 1, XC, S["y_done"])
                for t in range(q * JB, (q + 1) * JB):
                    m = t_.matmul(accC[1][:, 0:F], ones[:], xn[:, t, :], start=t == 0, stop=t == NT - 1)
            m.then_inc(S["sums_done"], 1)
            supertile(0, 0, first=True)
            with t_.Fori(0, NG // 2 - 1) as u:
                supertile(u * 2 + 1, 1)
                supertile(u * 2 + 2, 0)
            supertile(NG - 1, 1, last=True)

            def turn_weights():
                pe.wait_ge(S["w_in"], 16 * 12)
                for kb in range(KB):
                    m = t_.transpose(ps[1][:, kb * P:(kb + 1) * P], w_out[:, kb], ident[:])
                m.then_inc(S["w_turned"], 1)

            def join_weights():
                pe.wait_ge(S["w_copied"], 1)
                for kb in range(KB):
                    m = t_.matmul(ps[2][:, kb * P:(kb + 1) * P], w_outT[:, kb], w_lin, start=True, stop=True)
                m.then_inc(S["w_mult"], 1)

            def feature_mean():
                pe.wait_ge(S["featsum_done"], 1)
                t_.matmul(ps[3][:, 0:F], ones[:], featsum[:], start=True, stop=True).then_inc(S["ysum_done"], 1)

            def slot(s_, k, now, then, ok):
                def block(ch, between=None):
                    if now:
                        if ch == 0:
                            wait(pe, "acc_read", s_ + (NT - 1))
                            if isinstance(s_, int) and s_ < 2:
                                pe.wait_ge(S["summed"], s_ + (NT - 1))
                            wait(pe, "x1_done", s_ - 1)
                        early = isinstance(s_, int) and s_ == 0
                        products(s_ * NB + (R1 + ch), k % 2, ch, ch, F, S["y2_done"] if early else None, between)
                        if early and ch == 0:
                            turn_weights()
                        if early and ch == 2:
                            join_weights()
                            feature_mean()
                    elif between is not None:
                        between()

                c = k % 2
                if ok[1]:
                    pe.wait_ge(S["xn2_ready"], s_ - 1)
                    if ok[4]:
                        pe.wait_ge(S["y_read"], s_ - 4)
                    t_.transpose(ps[0][:, 0:P], xn2[:, c], ident[:]).then_inc(S["p_xT"], 1)
                block(0)
                if ok[1]:
                    pe.wait_ge(S["xT_ready"], s_ - 1)
                    if ok[3]:
                        pe.wait_ge(S["exp_done"], s_ - 3)
                    if ok[4]:
                        pe.wait_ge(S["yT_ready"], s_ - 4)
                    t_.matmul(ps[2][:, 0:DI + NH], xn2T, w_zdt, start=True, stop=True)
                    for cb in range(CB):
                        m = t_.matmul(ps[3][:, cb * P:(cb + 1) * P], w_xbc[:, cb * P:(cb + 1) * P], xn2T, start=True, stop=True)
                    m.then_inc(S["p_in"], 1)
                if ok[3]:
                    pe.wait_ge(S["mix_ready"], s_ - 3)
                    pe.wait_ge(S["xdt_ready"], s_ - 3)
                    pe.wait_ge(S["cT_ready"], s_ - 3)
                    if ok[4]:
                        pe.wait_ge(S["st_done"], s_ - 4)
                    for h in range(NH):
                        t_.matmul(ps[0][:, h * HD:(h + 1) * HD], wmix[:, h], xdt[:, h * HD:(h + 1) * HD], start=True, stop=True)
                    t_.matmul(ps[0][:, DI:2 * DI], cT[0:DS], state[0:DS, c], start=True, stop=True)
                    if ok[4]:
                        pe.wait_ge(S["out_done"], s_ - 4)
                    t_.matmul(ps[1][0:DS, 0:DI], xl[:, DI:DI + DS], xdtd, start=True, stop=True).then_inc(S["p_y"], 1)
                block(1)
                if ok[2]:
                    c3 = (k - 3) % 2
                    da = tiny[:, 2 + c3, NH:2 * NH]
                    pe.wait_ge(S["dam_ready"], s_ - 2)
                    if ok[1]:
                        pe.wait_ge(S["in_read"], s_ - 1)
                    pe.wait_ge(S["conv_ready"], s_ - 2)
                    t_.matmul(ps[2][:, 0:NH], upto, da, start=True, stop=True)
                    t_.matmul(ps[2][:, NH:2 * NH], ones[:], da, start=True, stop=True)
                    t_.matmul(ps[3][:, 0:NH * P], after, dam.rearrange("p h w -> p (h w)"), start=True, stop=True)
                    for cb in range(CB):
                        m = t_.transpose(ps[2][:, (cb + 1) * P:(cb + 2) * P], xbc[:, c3, cb], ident[:])
                    m.then_inc(S["p_cum"], 1)
                block(2)
                if ok[2]:
                    pe.wait_ge(S["xl_ready"], s_ - 2)
                    if ok[3]:
                        pe.wait_ge(S["st_done"], s_ - 3)
                    t_.matmul(ps[1][0:DS, 2 * P:3 * P], xl[:, DI + DS:DI + 2 * DS], ident[:], start=True, stop=True).then_inc(S["p_ct"], 1)

                def turn_y():
                    if ok[3]:
                        pe.wait_ge(S["yg_ready"], s_ - 3)
                        if ok[2]:
                            pe.wait_ge(S["exp_done"], s_ - 2)
                        for kb in range(KB):
                            m = t_.transpose(ps[3][:, kb * P:(kb + 1) * P], yg[:, kb * P:(kb + 1) * P], ident[:])
                        m.then_inc(S["p_yT"], 1)

                block(3, turn_y)
                if ok[2]:
                    pe.wait_ge(S["cT_ready"], s_ - 2)
                    if ok[3]:
                        pe.wait_ge(S["st_done"], s_ - 3)
                    t_.matmul(ps[1][:, 0:P], xbc[0:DS, (k - 3) % 2, CB - 1, :], cT[0:DS], start=True, stop=True).then_inc(S["p_g"], 1)
                if ok[3]:
                    pe.wait_ge(S["yT_ready"], s_ - 3)
                    pe.wait_ge(S["st_done"], s_ - 3)
                    for kb in range(KB):
                        m = t_.matmul(ps[1][:, P:P + F], yT[:, kb], w_comb[:, kb], start=kb == 0, stop=kb == KB - 1)
                    m.then_inc(S["p_o"], 1)

            schedule(t_, slot)


_INS = ['x', 'adj', 'L0_gnn_h0', 'L0_gnn_a', 'L0_gnn_temp', 'L0_ffn_W_in', 'L0_ffn_conv_w', 'L0_ffn_conv_b',
        'L0_ffn_dt_bias', 'L0_ffn_A_log', 'L0_ffn_D', 'L0_ffn_norm_w', 'L0_ffn_W_out', 'L0_ffn_W_lin', 'L0_ffn_b_lin']
_OUTS = [((4096, 128), 'float32')]


def kernel(**inputs):
    import numpy as _np
    import concourse.bacc as _bacc
    from concourse import mybir as _mybir
    from concourse.bass_utils import run_bass_kernel_spmd as _run

    nc = _bacc.Bacc("TRN2", target_bir_lowering=False, num_devices=1)
    arrays, args = {}, []
    for name in _INS:
        arr = _np.ascontiguousarray(inputs[name])
        arrays[f"in_{name}_dram"] = arr
        args.append(nc.dram_tensor(f"in_{name}_dram", arr.shape, _mybir.dt.from_np(arr.dtype), kind="ExternalInput").ap())
    for i, (shape, dtype) in enumerate(_OUTS):
        dt = _mybir.dt.from_np(_np.dtype(dtype))
        args.append(nc.dram_tensor(f"out_{i}_dram", shape, dt, kind="ExternalOutput").ap())
    gnn_ffn_kernel(nc, *args)
    r = _run(nc, [arrays], core_ids=[0])
    return r.results[0]["out_0_dram"]
```
